# Optimizing a Trainium2 kernel written in Bass

```python
import numpy as np
import jax
import jax.numpy as jnp

def _softmax(x, axis=-1):
    return jax.nn.softmax(x, axis=axis)

def _gelu(x):
    return jax.nn.gelu(x, approximate=True)

def _silu(x):
    return jax.nn.silu(x)

def _sigmoid(x):
    return jax.nn.sigmoid(x)

def _layernorm(x, axis=-1, eps=1e-05):
    m = jnp.mean(x, axis=axis, keepdims=True)
    v = jnp.var(x, axis=axis, keepdims=True)
    return (x - m) / jnp.sqrt(v + eps)

def _scatter_add(tgt, idx, src, axis=0):
    return tgt.at[idx].add(src)

def _segment_sum(src, seg, n):
    return jax.ops.segment_sum(src, seg, n)
kernel_name = 'mk_gps_d4_gnn_r32_cae509'

def setup_inputs(seed: int=0):
    np.random.seed(seed)
    _w = jnp.asarray

    def _rec_inputs():
        import jax
        import jax.numpy as jnp
        _gk = jax.random.key(seed)
        x = -0.0002117 + 1 * jax.random.normal(jax.random.fold_in(_gk, 1), (3125, 256), jnp.float32)
        src = jax.random.randint(jax.random.fold_in(_gk, 2), (50000,), 0, 3125, jnp.int32)
        dst = jax.random.randint(jax.random.fold_in(_gk, 3), (50000,), 0, 3125, jnp.int32)
        _o = jnp.argsort(dst, stable=True)
        src = src[_o]
        dst = dst[_o]
        edge_attr_2 = jax.random.uniform(jax.random.fold_in(_gk, 12), (50000, 2), jnp.float32, 0.0, 1)
        edge_type_2 = jax.random.randint(jax.random.fold_in(_gk, 14), (50000,), 0, 2, jnp.int32)
        return (x, src, dst, edge_attr_2, edge_type_2)
    x, src, dst, edge_attr_2, edge_type_2 = _rec_inputs()

    def _L0_gnn_setup():
        import jax, jax.numpy as jnp
        import numpy as np
        N_NODES = 3125
        N_EDGES = 50000
        IN_FEATS = 256
        OUT_FEATS = 64
        NUM_HEADS = 4
        key = jax.random.key(seed)
        k_h, k_adj, k_dir, k_wf, k_wr, k_af = jax.random.split(key, 6)
        h = jax.random.normal(k_h, (N_NODES, IN_FEATS), dtype=jnp.float32)
        adj = jax.random.randint(k_adj, (2, N_EDGES), 0, N_NODES, dtype=jnp.int64)
        bit = jax.random.randint(k_dir, (N_EDGES,), 0, 2).astype(jnp.float32)
        direction = jnp.stack([bit, 1.0 - bit], axis=1)
        s_w = float(np.sqrt(6.0 / (IN_FEATS + OUT_FEATS)))
        s_a = float(np.sqrt(6.0 / (NUM_HEADS + OUT_FEATS)))
        W_forward = jax.random.uniform(k_wf, (OUT_FEATS, IN_FEATS), jnp.float32, -s_w, s_w)
        W_reverse = jax.random.uniform(k_wr, (OUT_FEATS, IN_FEATS), jnp.float32, -s_w, s_w)
        attn_forward = jax.random.uniform(k_af, (1, NUM_HEADS, OUT_FEATS), jnp.float32, -s_a, s_a)
        return {'h': h, 'adj': adj, 'direction': direction, 'W_forward': W_forward, 'W_reverse': W_reverse, 'attn_forward': attn_forward}
    _L0_gnn_all = _L0_gnn_setup()
    _L0_gnn_in = {k: v for k, v in _L0_gnn_all.items() if k in ('W_forward', 'W_reverse', 'attn_forward')}
    del _L0_gnn_all

    def _L0_mix_setup():
        import jax, jax.numpy as jnp
        import numpy as np
        NUM_HEADS = 8
        key = jax.random.key(seed)
        ks = jax.random.split(key, 5)
        B, N, C = (8, 512, 256)
        x = jax.random.normal(ks[0], (B, N, C), dtype=jnp.float32)
        Wq = jax.random.normal(ks[1], (C, C), dtype=jnp.float32) * 0.02
        Wkv = jax.random.normal(ks[2], (2 * C, C), dtype=jnp.float32) * 0.02
        Wproj = jax.random.normal(ks[3], (C, C), dtype=jnp.float32) * 0.02
        bproj = jnp.zeros((C,), dtype=jnp.float32)
        return {'x': x, 'Wq': Wq, 'Wkv': Wkv, 'Wproj': Wproj, 'bproj': bproj}
    _L0_mix_all = _L0_mix_setup()
    _L0_mix_in = {k: v for k, v in _L0_mix_all.items() if k in ('Wq', 'Wkv', 'Wproj', 'bproj')}
    del _L0_mix_all

    def _L0_ffn_setup():
        import jax, jax.numpy as jnp
        import numpy as np
        E, D, H, TOP_K = (6, 256, 256, 2)
        ROUTER_H = D // 2
        key = jax.random.key(seed)
        ks = jax.random.split(key, 12)
        s = 1.0 / np.sqrt(D)
        sh = 1.0 / np.sqrt(H)
        sr = 1.0 / np.sqrt(ROUTER_H)
        return {'features': jax.random.normal(ks[0], (8, 128, D), dtype=jnp.float32), 'router_w1': jax.random.uniform(ks[1], (D, ROUTER_H), jnp.float32, -s, s), 'router_b1': jnp.zeros((ROUTER_H,), jnp.float32), 'router_w2': jax.random.uniform(ks[2], (ROUTER_H, E), jnp.float32, -sr, sr), 'router_b2': jnp.zeros((E,), jnp.float32), 'expert_w1': jax.random.uniform(ks[3], (E, D, H), jnp.float32, -s, s), 'expert_b1': jnp.zeros((E, H), jnp.float32), 'expert_w2': jax.random.uniform(ks[4], (E, H, H), jnp.float32, -sh, sh), 'expert_b2': jnp.zeros((E, H), jnp.float32), 'expert_w3': jax.random.uniform(ks[5], (E, H, D), jnp.float32, -sh, sh), 'expert_b3': jnp.zeros((E, D), jnp.float32)}
    _L0_ffn_all = _L0_ffn_setup()
    _L0_ffn_in = {k: v for k, v in _L0_ffn_all.items() if k in ('router_w1', 'router_b1', 'router_w2', 'router_b2', 'expert_w1', 'expert_b1', 'expert_w2', 'expert_b2', 'expert_w3', 'expert_b3')}
    del _L0_ffn_all

    def _L1_gnn_setup():
        import jax, jax.numpy as jnp
        import numpy as np
        HIDDEN = 256
        HEADS = 8
        HEAD_DIM = HIDDEN // HEADS
        N_NODES = 50000
        N_EDGES = 25000
        key = jax.random.key(seed)
        ks = jax.random.split(key, 12)
        h = jax.random.normal(ks[0], (N_NODES, HIDDEN), dtype=jnp.float32)
        row = jax.random.randint(ks[1], (N_EDGES,), 0, N_NODES, dtype=jnp.int64 if jax.config.jax_enable_x64 else jnp.int32)
        col = jax.random.randint(ks[2], (N_EDGES,), 0, N_NODES, dtype=jnp.int64 if jax.config.jax_enable_x64 else jnp.int32)

        def lin(kw, kb):
            W = jax.random.normal(kw, (HIDDEN, HIDDEN), dtype=jnp.float32) * 0.02
            b = jax.random.normal(kb, (HIDDEN,), dtype=jnp.float32) * 0.02
            return (W, b)
        Wq, bq = lin(ks[3], ks[4])
        Wk, bk = lin(ks[5], ks[6])
        Wv, bv = lin(ks[7], ks[8])
        Wo, bo = lin(ks[9], ks[10])
        return {'h': h, 'row': row, 'col': col, 'Wq': Wq, 'bq': bq, 'Wk': Wk, 'bk': bk, 'Wv': Wv, 'bv': bv, 'Wo': Wo, 'bo': bo}
    _L1_gnn_all = _L1_gnn_setup()
    _L1_gnn_in = {k: v for k, v in _L1_gnn_all.items() if k in ('Wq', 'bq', 'Wk', 'bk', 'Wv', 'bv', 'Wo', 'bo')}
    del _L1_gnn_all

    def _L1_mix_setup():
        import jax, jax.numpy as jnp
        import numpy as np
        HEADS = 4
        DIM_HEAD = 32
        key = jax.random.key(seed)
        k1, k2, k3 = jax.random.split(key, 3)
        B, L, D = (16, 256, 256)
        hidden = HEADS * DIM_HEAD
        x = jax.random.normal(k1, (B, L, D), dtype=jnp.float32)
        W_qkv = jax.random.normal(k2, (D, 3 * hidden), dtype=jnp.float32) * D ** (-0.5)
        W_out = jax.random.normal(k3, (hidden, D), dtype=jnp.float32) * hidden ** (-0.5)
        b_out = jnp.zeros((D,), dtype=jnp.float32)
        return {'x': x, 'W_qkv': W_qkv, 'W_out': W_out, 'b_out': b_out}
    _L1_mix_all = _L1_mix_setup()
    _L1_mix_in = {k: v for k, v in _L1_mix_all.items() if k in ('W_qkv', 'W_out', 'b_out')}
    del _L1_mix_all

    def _L1_ffn_setup():
        import jax, jax.numpy as jnp
        import numpy as np
        B, S, D = (8, 128, 256)
        H = 4 * D
        CAPACITY = 0.5
        key = jax.random.key(seed)
        ks = jax.random.split(key, 6)
        x = jax.random.normal(ks[0], (B, S, D), dtype=jnp.float32)
        attention_mask = jnp.zeros((B, 1, 1, S), dtype=jnp.float32)
        wr = jax.random.normal(ks[1], (D, 1), dtype=jnp.float32) * 0.02
        br = jnp.zeros((1,), dtype=jnp.float32)
        w1 = jax.random.normal(ks[2], (D, H), dtype=jnp.float32) * 0.02
        b1 = jnp.zeros((H,), dtype=jnp.float32)
        w2 = jax.random.normal(ks[3], (H, D), dtype=jnp.float32) * 0.02
        b2 = jnp.zeros((D,), dtype=jnp.float32)
        return {'x': x, 'attention_mask': attention_mask, 'wr': wr, 'br': br, 'w1': w1, 'b1': b1, 'w2': w2, 'b2': b2}
    _L1_ffn_all = _L1_ffn_setup()
    _L1_ffn_in = {k: v for k, v in _L1_ffn_all.items() if k in ('attention_mask', 'wr', 'br', 'w1', 'b1', 'w2', 'b2')}
    del _L1_ffn_all

    def _L2_gnn_setup():
        import jax, jax.numpy as jnp
        import numpy as np
        N_NODES = 10000
        N_EDGES = 10000
        D = 256
        D_OUT = 256
        NUM_REL = 2
        key = jax.random.key(seed)
        ks = jax.random.split(key, 16)
        s = 1.0 / np.sqrt(D)
        inp = {}
        inp['feat'] = jax.random.normal(ks[0], (N_NODES, D), dtype=jnp.float32)
        inp['src'] = jax.random.randint(ks[1], (N_EDGES,), 0, N_NODES, dtype=jnp.int32)
        inp['dst'] = jax.random.randint(ks[2], (N_EDGES,), 0, N_NODES, dtype=jnp.int32)
        inp['rel'] = jax.random.randint(ks[3], (N_EDGES,), 0, NUM_REL, dtype=jnp.int32)
        inp['W_rel'] = jax.random.normal(ks[4], (NUM_REL, D, D), dtype=jnp.float32) * s
        inp['b_rel'] = jax.random.normal(ks[5], (NUM_REL, D), dtype=jnp.float32) * s
        inp['W_ih'] = jax.random.normal(ks[6], (4 * D, D), dtype=jnp.float32) * s
        inp['b_ih'] = jax.random.normal(ks[7], (4 * D,), dtype=jnp.float32) * s
        inp['b_hh'] = jax.random.normal(ks[8], (4 * D,), dtype=jnp.float32) * s
        h = D // 2
        inp['W1'] = jax.random.normal(ks[9], (h, D), dtype=jnp.float32) * s
        inp['b1'] = jax.random.normal(ks[10], (h,), dtype=jnp.float32) * s
        inp['W2'] = jax.random.normal(ks[11], (h, h), dtype=jnp.float32) * (1.0 / np.sqrt(h))
        inp['b2'] = jax.random.normal(ks[12], (h,), dtype=jnp.float32) * (1.0 / np.sqrt(h))
        inp['W3'] = jax.random.normal(ks[13], (D_OUT, h), dtype=jnp.float32) * (1.0 / np.sqrt(h))
        inp['b3'] = jax.random.normal(ks[14], (D_OUT,), dtype=jnp.float32) * (1.0 / np.sqrt(h))
        return inp
    _L2_gnn_all = _L2_gnn_setup()
    _L2_gnn_in = {k: v for k, v in _L2_gnn_all.items() if k in ('W_rel', 'b_rel', 'W_ih', 'b_ih', 'b_hh', 'W1', 'b1', 'W2', 'b2', 'W3', 'b3')}
    del _L2_gnn_all

    def _L2_mix_setup():
        import jax, jax.numpy as jnp
        import numpy as np
        HEADS = 8
        DIM_HEAD = 32
        SCALE = DIM_HEAD ** (-0.5)
        EPS = 1e-05

        def _layernorm_gamma(x, gamma):
            mu = jnp.mean(x, axis=-1, keepdims=True)
            var = jnp.var(x, axis=-1, keepdims=True)
            return (x - mu) * jax.lax.rsqrt(var + EPS) * gamma
        key = jax.random.key(seed)
        k1, k2, k3 = jax.random.split(key, 3)
        B, N, D = (8, 512, 256)
        hidden = HEADS * DIM_HEAD
        x = jax.random.normal(k1, (B, N, D), dtype=jnp.float32)
        Wqkv = jax.random.normal(k2, (D, 3 * hidden), dtype=jnp.float32) * D ** (-0.5)
        Wout = jax.random.normal(k3, (hidden, D), dtype=jnp.float32) * hidden ** (-0.5)
        gamma = jnp.ones((D,), dtype=jnp.float32)
        return {'x': x, 'Wqkv': Wqkv, 'Wout': Wout, 'gamma': gamma}
    _L2_mix_all = _L2_mix_setup()
    _L2_mix_in = {k: v for k, v in _L2_mix_all.items() if k in ('Wqkv', 'Wout', 'gamma')}
    del _L2_mix_all

    def _L2_ffn_setup():
        import jax, jax.numpy as jnp
        import numpy as np
        NUM_EXPERTS = 8
        TOP_K = 2
        B, S, D = (8, 256, 256)

        def _moe(tokens, router_w, w1, b1, w2, b2):
            N = tokens.shape[0]
            E = router_w.shape[0]
            logits = tokens.astype(jnp.float32) @ router_w.astype(jnp.float32).T
            probs = jax.nn.softmax(logits, axis=-1)
            rw, re = jax.lax.top_k(probs, TOP_K)
            if TOP_K > 1:
                rw = rw / jnp.maximum(rw.sum(-1, keepdims=True), 1e-12)
            rw = rw.astype(tokens.dtype)
            combine = jnp.zeros((N, E), tokens.dtype).at[jnp.arange(N)[:, None], re].set(rw)
            out = tokens
            for e in range(E):
                h = jax.nn.gelu(tokens @ w1[e] + b1[e], approximate=False)
                y = h @ w2[e] + b2[e]
                out = out + combine[:, e:e + 1] * y
            return out
        key = jax.random.key(seed)
        ks = jax.random.split(key, 4)
        scale = 1.0 / np.sqrt(D).astype(np.float32)
        return {'input_embeddings': jax.random.normal(ks[0], (B, S, D), jnp.float32), 'router_w': jax.random.normal(ks[1], (NUM_EXPERTS, D), jnp.float32) * scale, 'w1': jax.random.normal(ks[2], (NUM_EXPERTS, D, D), jnp.float32) * scale, 'b1': jnp.zeros((NUM_EXPERTS, D), jnp.float32), 'w2': jax.random.normal(ks[3], (NUM_EXPERTS, D, D), jnp.float32) * scale, 'b2': jnp.zeros((NUM_EXPERTS, D), jnp.float32)}
    _L2_ffn_all = _L2_ffn_setup()
    _L2_ffn_in = {k: v for k, v in _L2_ffn_all.items() if k in ('router_w', 'w1', 'b1', 'w2', 'b2')}
    del _L2_ffn_all

    def _L3_gnn_setup():
        import jax, jax.numpy as jnp
        import numpy as np
        N = 50000
        E = 25000
        F_DIM = 256
        H = 4
        C = 64
        SLOPE = 0.2

        def gat_layer(x, src, dst, W, a_src, a_dst, bias, heads, out_ch):
            n = x.shape[0]
            xW = (x @ W).reshape(n, heads, out_ch)
            alpha_s = jnp.sum(xW * a_src, axis=-1)
            alpha_d = jnp.sum(xW * a_dst, axis=-1)
            e = jax.nn.leaky_relu(alpha_s[src] + alpha_d[dst], SLOPE)
            m = jax.ops.segment_max(e, dst, num_segments=n)
            w = jnp.exp(e - m[dst])
            z = jax.ops.segment_sum(w, dst, num_segments=n)
            alpha = w / z[dst]
            out = jax.ops.segment_sum(xW[src] * alpha[:, :, None], dst, num_segments=n)
            return out.reshape(n, heads * out_ch) + bias
        key = jax.random.key(seed)
        ks = jax.random.split(key, 11)
        s = 0.05
        return {'x': jax.random.normal(ks[0], (N, F_DIM), jnp.float32), 'edge_index': jax.random.randint(ks[1], (2, E), 0, N), 'W1': jax.random.normal(ks[2], (F_DIM, H * C), jnp.float32) * s, 'a_src1': jax.random.normal(ks[3], (H, C), jnp.float32) * s, 'a_dst1': jax.random.normal(ks[4], (H, C), jnp.float32) * s, 'b1': jnp.zeros((H * C,), jnp.float32), 'W2': jax.random.normal(ks[5], (H * C, F_DIM), jnp.float32) * s, 'a_src2': jax.random.normal(ks[6], (1, F_DIM), jnp.float32) * s, 'a_dst2': jax.random.normal(ks[7], (1, F_DIM), jnp.float32) * s, 'b2': jnp.zeros((F_DIM,), jnp.float32)}
    _L3_gnn_all = _L3_gnn_setup()
    _L3_gnn_in = {k: v for k, v in _L3_gnn_all.items() if k in ('W1', 'a_src1', 'a_dst1', 'b1', 'W2', 'a_src2', 'a_dst2', 'b2')}
    del _L3_gnn_all

    def _L3_mix_setup():
        import jax, jax.numpy as jnp
        import numpy as np
        NHEAD = 8
        ATT_EPS = 1e-06
        LN_EPS = 1e-05

        def _layernorm(x, g, b):
            mu = jnp.mean(x, axis=-1, keepdims=True)
            var = jnp.mean(jnp.square(x - mu), axis=-1, keepdims=True)
            return (x - mu) * jax.lax.rsqrt(var + LN_EPS) * g + b
        key = jax.random.key(seed)
        ks = jax.random.split(key, 7)
        N, L, C = (4, 512, 256)
        s = 1.0 / np.sqrt(C)
        return {'x': jax.random.normal(ks[0], (N, L, C), jnp.float32), 'Wq': jax.random.normal(ks[1], (C, C), jnp.float32) * s, 'Wk': jax.random.normal(ks[2], (C, C), jnp.float32) * s, 'Wv': jax.random.normal(ks[3], (C, C), jnp.float32) * s, 'Wm': jax.random.normal(ks[4], (C, C), jnp.float32) * s, 'W1': jax.random.normal(ks[5], (2 * C, 2 * C), jnp.float32) * (1.0 / np.sqrt(2 * C)), 'W2': jax.random.normal(ks[6], (2 * C, C), jnp.float32) * (1.0 / np.sqrt(2 * C)), 'g1': jnp.ones((C,), jnp.float32), 'b1': jnp.zeros((C,), jnp.float32), 'g2': jnp.ones((C,), jnp.float32), 'b2': jnp.zeros((C,), jnp.float32)}
    _L3_mix_all = _L3_mix_setup()
    _L3_mix_in = {k: v for k, v in _L3_mix_all.items() if k in ('Wq', 'Wk', 'Wv', 'Wm', 'W1', 'W2', 'g1', 'b1', 'g2', 'b2')}
    del _L3_mix_all

    def _L3_ffn_setup():
        import math
        import jax, jax.numpy as jnp
        import numpy as np
        CAPACITY_FACTOR = 1.25
        key = jax.random.key(seed)
        ks = jax.random.split(key, 5)
        B, L, D, F, E = (8, 256, 256, 1024, 8)
        h = jax.random.normal(ks[0], (B, L, D), dtype=jnp.float32)
        gate_w = jax.random.normal(ks[1], (D, E), dtype=jnp.float32) * 0.02
        gate_b = jnp.zeros((E,), dtype=jnp.float32)
        w1 = jax.random.normal(ks[2], (E, D, F), dtype=jnp.float32) * (1.0 / math.sqrt(D))
        b1 = jnp.zeros((E, F), dtype=jnp.float32)
        w2 = jax.random.normal(ks[3], (E, F, D), dtype=jnp.float32) * (1.0 / math.sqrt(F))
        b2 = jnp.zeros((E, D), dtype=jnp.float32)
        return {'h': h, 'gate_w': gate_w, 'gate_b': gate_b, 'w1': w1, 'b1': b1, 'w2': w2, 'b2': b2}
    _L3_ffn_all = _L3_ffn_setup()
    _L3_ffn_in = {k: v for k, v in _L3_ffn_all.items() if k in ('gate_w', 'gate_b', 'w1', 'b1', 'w2', 'b2')}
    del _L3_ffn_all
    return {'x': x, 'src': src, 'dst': dst, 'edge_attr_2': edge_attr_2, 'edge_type_2': edge_type_2, 'L0_gnn_W_forward': _L0_gnn_in['W_forward'], 'L0_gnn_W_reverse': _L0_gnn_in['W_reverse'], 'L0_gnn_attn_forward': _L0_gnn_in['attn_forward'], 'L0_mix_Wq': _L0_mix_in['Wq'], 'L0_mix_Wkv': _L0_mix_in['Wkv'], 'L0_mix_Wproj': _L0_mix_in['Wproj'], 'L0_mix_bproj': _L0_mix_in['bproj'], 'L0_ffn_router_w1': _L0_ffn_in['router_w1'], 'L0_ffn_router_b1': _L0_ffn_in['router_b1'], 'L0_ffn_router_w2': _L0_ffn_in['router_w2'], 'L0_ffn_router_b2': _L0_ffn_in['router_b2'], 'L0_ffn_expert_w1': _L0_ffn_in['expert_w1'], 'L0_ffn_expert_b1': _L0_ffn_in['expert_b1'], 'L0_ffn_expert_w2': _L0_ffn_in['expert_w2'], 'L0_ffn_expert_b2': _L0_ffn_in['expert_b2'], 'L0_ffn_expert_w3': _L0_ffn_in['expert_w3'], 'L0_ffn_expert_b3': _L0_ffn_in['expert_b3'], 'L1_gnn_Wq': _L1_gnn_in['Wq'], 'L1_gnn_bq': _L1_gnn_in['bq'], 'L1_gnn_Wk': _L1_gnn_in['Wk'], 'L1_gnn_bk': _L1_gnn_in['bk'], 'L1_gnn_Wv': _L1_gnn_in['Wv'], 'L1_gnn_bv': _L1_gnn_in['bv'], 'L1_gnn_Wo': _L1_gnn_in['Wo'], 'L1_gnn_bo': _L1_gnn_in['bo'], 'L1_mix_W_qkv': _L1_mix_in['W_qkv'], 'L1_mix_W_out': _L1_mix_in['W_out'], 'L1_mix_b_out': _L1_mix_in['b_out'], 'L1_ffn_attention_mask': _L1_ffn_in['attention_mask'], 'L1_ffn_wr': _L1_ffn_in['wr'], 'L1_ffn_br': _L1_ffn_in['br'], 'L1_ffn_w1': _L1_ffn_in['w1'], 'L1_ffn_b1': _L1_ffn_in['b1'], 'L1_ffn_w2': _L1_ffn_in['w2'], 'L1_ffn_b2': _L1_ffn_in['b2'], 'L2_gnn_W_rel': _L2_gnn_in['W_rel'], 'L2_gnn_b_rel': _L2_gnn_in['b_rel'], 'L2_gnn_W_ih': _L2_gnn_in['W_ih'], 'L2_gnn_b_ih': _L2_gnn_in['b_ih'], 'L2_gnn_b_hh': _L2_gnn_in['b_hh'], 'L2_gnn_W1': _L2_gnn_in['W1'], 'L2_gnn_b1': _L2_gnn_in['b1'], 'L2_gnn_W2': _L2_gnn_in['W2'], 'L2_gnn_b2': _L2_gnn_in['b2'], 'L2_gnn_W3': _L2_gnn_in['W3'], 'L2_gnn_b3': _L2_gnn_in['b3'], 'L2_mix_Wqkv': _L2_mix_in['Wqkv'], 'L2_mix_Wout': _L2_mix_in['Wout'], 'L2_mix_gamma': _L2_mix_in['gamma'], 'L2_ffn_router_w': _L2_ffn_in['router_w'], 'L2_ffn_w1': _L2_ffn_in['w1'], 'L2_ffn_b1': _L2_ffn_in['b1'], 'L2_ffn_w2': _L2_ffn_in['w2'], 'L2_ffn_b2': _L2_ffn_in['b2'], 'L3_gnn_W1': _L3_gnn_in['W1'], 'L3_gnn_a_src1': _L3_gnn_in['a_src1'], 'L3_gnn_a_dst1': _L3_gnn_in['a_dst1'], 'L3_gnn_b1': _L3_gnn_in['b1'], 'L3_gnn_W2': _L3_gnn_in['W2'], 'L3_gnn_a_src2': _L3_gnn_in['a_src2'], 'L3_gnn_a_dst2': _L3_gnn_in['a_dst2'], 'L3_gnn_b2': _L3_gnn_in['b2'], 'L3_mix_Wq': _L3_mix_in['Wq'], 'L3_mix_Wk': _L3_mix_in['Wk'], 'L3_mix_Wv': _L3_mix_in['Wv'], 'L3_mix_Wm': _L3_mix_in['Wm'], 'L3_mix_W1': _L3_mix_in['W1'], 'L3_mix_W2': _L3_mix_in['W2'], 'L3_mix_g1': _L3_mix_in['g1'], 'L3_mix_b1': _L3_mix_in['b1'], 'L3_mix_g2': _L3_mix_in['g2'], 'L3_mix_b2': _L3_mix_in['b2'], 'L3_ffn_gate_w': _L3_ffn_in['gate_w'], 'L3_ffn_gate_b': _L3_ffn_in['gate_b'], 'L3_ffn_w1': _L3_ffn_in['w1'], 'L3_ffn_b1': _L3_ffn_in['b1'], 'L3_ffn_w2': _L3_ffn_in['w2'], 'L3_ffn_b2': _L3_ffn_in['b2']}

def reference(x, src, dst, edge_attr_2, edge_type_2, L0_gnn_W_forward, L0_gnn_W_reverse, L0_gnn_attn_forward, L0_mix_Wq, L0_mix_Wkv, L0_mix_Wproj, L0_mix_bproj, L0_ffn_router_w1, L0_ffn_router_b1, L0_ffn_router_w2, L0_ffn_router_b2, L0_ffn_expert_w1, L0_ffn_expert_b1, L0_ffn_expert_w2, L0_ffn_expert_b2, L0_ffn_expert_w3, L0_ffn_expert_b3, L1_gnn_Wq, L1_gnn_bq, L1_gnn_Wk, L1_gnn_bk, L1_gnn_Wv, L1_gnn_bv, L1_gnn_Wo, L1_gnn_bo, L1_mix_W_qkv, L1_mix_W_out, L1_mix_b_out, L1_ffn_attention_mask, L1_ffn_wr, L1_ffn_br, L1_ffn_w1, L1_ffn_b1, L1_ffn_w2, L1_ffn_b2, L2_gnn_W_rel, L2_gnn_b_rel, L2_gnn_W_ih, L2_gnn_b_ih, L2_gnn_b_hh, L2_gnn_W1, L2_gnn_b1, L2_gnn_W2, L2_gnn_b2, L2_gnn_W3, L2_gnn_b3, L2_mix_Wqkv, L2_mix_Wout, L2_mix_gamma, L2_ffn_router_w, L2_ffn_w1, L2_ffn_b1, L2_ffn_w2, L2_ffn_b2, L3_gnn_W1, L3_gnn_a_src1, L3_gnn_a_dst1, L3_gnn_b1, L3_gnn_W2, L3_gnn_a_src2, L3_gnn_a_dst2, L3_gnn_b2, L3_mix_Wq, L3_mix_Wk, L3_mix_Wv, L3_mix_Wm, L3_mix_W1, L3_mix_W2, L3_mix_g1, L3_mix_b1, L3_mix_g2, L3_mix_b2, L3_ffn_gate_w, L3_ffn_gate_b, L3_ffn_w1, L3_ffn_b1, L3_ffn_w2, L3_ffn_b2):
    import jax
    import jax.numpy as jnp

    def _L0_gnn_ref(h, adj, direction, W_forward, W_reverse, attn_forward):
        import jax, jax.numpy as jnp
        import numpy as np
        N_NODES = 3125
        N_EDGES = 50000
        IN_FEATS = 256
        OUT_FEATS = 64
        NUM_HEADS = 4
        N = h.shape[0]
        H = attn_forward.shape[1]
        h_fwd = h @ W_forward.T
        h_rev = h @ W_reverse.T
        src, dst = (adj[0], adj[1])
        messages = h_fwd[src] * direction[:, 0:1] + h_rev[src] * direction[:, 1:2]
        scores = jnp.einsum('ef,hf->eh', messages, attn_forward[0])
        scores = jax.nn.leaky_relu(scores, negative_slope=0.2)
        exp_scores = jnp.exp(scores - scores.max(axis=0, keepdims=True))
        sum_exp = jax.ops.segment_sum(exp_scores, dst, num_segments=N)
        norm = exp_scores / (sum_exp[dst] + 1e-10)
        outs = [jax.ops.segment_sum(messages * norm[:, hd:hd + 1], dst, num_segments=N) for hd in range(H)]
        out = jnp.stack(outs, axis=1)
        return out.reshape(N, -1)

    def _L0_mix_ref(x, Wq, Wkv, Wproj, bproj):
        import jax, jax.numpy as jnp
        import numpy as np
        NUM_HEADS = 8
        B, N, C = x.shape
        h = NUM_HEADS
        d = C // h
        q = jnp.einsum('bnc,oc->bno', x, Wq).reshape(B, N, h, d).transpose(0, 2, 1, 3)
        kv = jnp.einsum('bnc,oc->bno', x, Wkv).reshape(B, N, 2, h, d)
        k = kv[:, :, 0].transpose(0, 2, 1, 3)
        v = kv[:, :, 1].transpose(0, 2, 1, 3)
        q = jax.nn.elu(q) + 1.0
        k = jax.nn.elu(k) + 1.0
        k_sum = k.sum(axis=2)
        D_inv = 1.0 / jnp.maximum(jnp.einsum('bhnd,bhd->bhn', q, k_sum), 1e-06)
        context = jnp.einsum('bhnd,bhne->bhde', k, v)
        attn = jnp.einsum('bhnd,bhde->bhne', q, context) * D_inv[..., None]
        out = attn.transpose(0, 2, 1, 3).reshape(B, N, C)
        out = jnp.einsum('bnc,oc->bno', out, Wproj) + bproj
        return out

    def _L0_ffn_ref(features, router_w1, router_b1, router_w2, router_b2, expert_w1, expert_b1, expert_w2, expert_b2, expert_w3, expert_b3):
        import jax, jax.numpy as jnp
        import numpy as np
        E, D, H, TOP_K = (6, 256, 256, 2)
        ROUTER_H = D // 2
        rh = jax.nn.relu(features @ router_w1 + router_b1)
        expert_logits = jax.nn.softmax(rh @ router_w2 + router_b2, axis=-1)
        top_w, top_i = jax.lax.top_k(expert_logits, TOP_K)
        routing_weights = jax.nn.softmax(top_w, axis=-1)
        h1 = jax.nn.relu(jnp.einsum('bsd,edh->bseh', features, expert_w1) + expert_b1)
        h2 = jax.nn.relu(jnp.einsum('bseh,ehf->bsef', h1, expert_w2) + expert_b2)
        expert_out = jnp.einsum('bsef,efo->bseo', h2, expert_w3) + expert_b3
        sel = jnp.take_along_axis(expert_out, top_i[:, :, :, None], axis=2)
        combined = jnp.sum(sel * routing_weights[..., None], axis=2)
        return combined

    def _L1_gnn_ref(h, row, col, Wq, bq, Wk, bk, Wv, bv, Wo, bo):
        import jax, jax.numpy as jnp
        import numpy as np
        HIDDEN = 256
        HEADS = 8
        HEAD_DIM = HIDDEN // HEADS
        N_NODES = 50000
        N_EDGES = 25000
        N = h.shape[0]
        scaling = HEAD_DIM ** (-0.5)
        q = (h @ Wq.T + bq).reshape(N, HEAD_DIM, HEADS) * scaling
        k = (h @ Wk.T + bk).reshape(N, HEAD_DIM, HEADS)
        v = (h @ Wv.T + bv).reshape(N, HEAD_DIM, HEADS)
        s = jnp.einsum('edh,edh->eh', q[row], k[col])
        m = jax.ops.segment_max(s, row, num_segments=N)
        e = jnp.exp(s - m[row])
        z = jax.ops.segment_sum(e, row, num_segments=N)
        attn = e / z[row]
        out = jax.ops.segment_sum(attn[:, None, :] * v[col], row, num_segments=N)
        return out.reshape(N, -1) @ Wo.T + bo

    def _L1_mix_ref(x, W_qkv, W_out, b_out):
        import jax, jax.numpy as jnp
        import numpy as np
        HEADS = 4
        DIM_HEAD = 32
        B, L, D = x.shape
        scale = DIM_HEAD ** (-0.5)
        qkv = jnp.einsum('bld,df->blf', x, W_qkv)
        qkv = qkv.reshape(B, L, 3, HEADS, DIM_HEAD)
        q = jnp.transpose(qkv[:, :, 0], (0, 2, 1, 3)) * scale
        k = jax.nn.softmax(jnp.transpose(qkv[:, :, 1], (0, 2, 1, 3)), axis=2)
        v = jnp.transpose(qkv[:, :, 2], (0, 2, 1, 3))
        context = jnp.einsum('bhld,bhle->bhde', k, v)
        out = jnp.einsum('bhde,bhld->bhle', context, q)
        out = jnp.transpose(out, (0, 2, 1, 3)).reshape(B, L, HEADS * DIM_HEAD)
        return jnp.einsum('blf,fd->bld', out, W_out) + b_out

    def _L1_ffn_ref(x, attention_mask, wr, br, w1, b1, w2, b2):
        import jax, jax.numpy as jnp
        import numpy as np
        B, S, D = (8, 128, 256)
        H = 4 * D
        CAPACITY = 0.5
        b, s, d = x.shape
        weights = (jnp.einsum('bsd,do->bso', x, wr) + br)[..., 0]
        k = max(1, int(CAPACITY * s))
        kk = k - 1 if k > 1 else 1
        _, idx = jax.lax.top_k(weights, k)
        sel_idx = idx[:, :kk]
        sel = jnp.take_along_axis(x, sel_idx[:, :, None], axis=1)
        h = jax.nn.gelu(jnp.einsum('bkd,dh->bkh', sel, w1) + b1)
        y = jnp.einsum('bkh,hd->bkd', h, w2) + b2
        w_sel = jnp.take_along_axis(weights, sel_idx, axis=1)
        y = y * w_sel[..., None]
        batch_idx = jnp.arange(b)[:, None]
        processed = jnp.zeros_like(x).at[batch_idx, sel_idx].set(y)
        return processed + x

    def _L2_gnn_ref(feat, src, dst, rel, W_rel, b_rel, W_ih, b_ih, b_hh, W1, b1, W2, b2, W3, b3):
        import jax, jax.numpy as jnp
        import numpy as np
        N_NODES = 10000
        N_EDGES = 10000
        D = 256
        D_OUT = 256
        NUM_REL = 2
        n_nodes = feat.shape[0]
        S = feat[src]

        def edge_nn(x, W, b):
            h = jax.nn.relu(x @ W.T + b)
            return jax.nn.relu(h @ W.T + b)
        msgs = jnp.zeros_like(S)
        for r in range(W_rel.shape[0]):
            msgs = jnp.where((rel == r)[:, None], edge_nn(S, W_rel[r], b_rel[r]), msgs)
        agg = jax.ops.segment_sum(msgs, dst, num_segments=n_nodes)
        gates = agg @ W_ih.T + b_ih + b_hh
        i, f, g, o = jnp.split(gates, 4, axis=-1)
        c = jax.nn.sigmoid(i) * jnp.tanh(g)
        hn = jax.nn.sigmoid(o) * jnp.tanh(c)
        x = jax.nn.relu(hn @ W1.T + b1)
        x = jax.nn.relu(x @ W2.T + b2)
        return x @ W3.T + b3

    def _L2_mix_ref(x, Wqkv, Wout, gamma):
        import jax, jax.numpy as jnp
        import numpy as np
        HEADS = 8
        DIM_HEAD = 32
        SCALE = DIM_HEAD ** (-0.5)
        EPS = 1e-05

        def _layernorm_gamma(x, gamma):
            mu = jnp.mean(x, axis=-1, keepdims=True)
            var = jnp.var(x, axis=-1, keepdims=True)
            return (x - mu) * jax.lax.rsqrt(var + EPS) * gamma
        B, N, D = x.shape
        qkv = x @ Wqkv
        q, k, v = jnp.split(qkv, 3, axis=-1)

        def to_heads(t):
            return t.reshape(B, N, HEADS, DIM_HEAD).transpose(0, 2, 1, 3)
        q, k, v = map(to_heads, (q, k, v))
        q = jax.nn.softmax(q, axis=-1) * SCALE
        k = jax.nn.softmax(k, axis=2)
        context = jnp.einsum('bhnd,bhne->bhde', k, v)
        out = jnp.einsum('bhde,bhnd->bhne', context, q)
        out = out.transpose(0, 2, 1, 3).reshape(B, N, HEADS * DIM_HEAD)
        out = out @ Wout
        return _layernorm_gamma(out, gamma)

    def _L2_ffn_ref(input_embeddings, router_w, w1, b1, w2, b2):
        import jax, jax.numpy as jnp
        import numpy as np
        NUM_EXPERTS = 8
        TOP_K = 2
        B, S, D = (8, 256, 256)

        def _moe(tokens, router_w, w1, b1, w2, b2):
            N = tokens.shape[0]
            E = router_w.shape[0]
            logits = tokens.astype(jnp.float32) @ router_w.astype(jnp.float32).T
            probs = jax.nn.softmax(logits, axis=-1)
            rw, re = jax.lax.top_k(probs, TOP_K)
            if TOP_K > 1:
                rw = rw / jnp.maximum(rw.sum(-1, keepdims=True), 1e-12)
            rw = rw.astype(tokens.dtype)
            combine = jnp.zeros((N, E), tokens.dtype).at[jnp.arange(N)[:, None], re].set(rw)
            out = tokens
            for e in range(E):
                h = jax.nn.gelu(tokens @ w1[e] + b1[e], approximate=False)
                y = h @ w2[e] + b2[e]
                out = out + combine[:, e:e + 1] * y
            return out
        b, s, d = input_embeddings.shape
        tokens = input_embeddings.reshape(b * s, d)
        return _moe(tokens, router_w, w1, b1, w2, b2).reshape(b, s, d)

    def _L3_gnn_ref(x, edge_index, W1, a_src1, a_dst1, b1, W2, a_src2, a_dst2, b2):
        import jax, jax.numpy as jnp
        import numpy as np
        N = 50000
        E = 25000
        F_DIM = 256
        H = 4
        C = 64
        SLOPE = 0.2

        def gat_layer(x, src, dst, W, a_src, a_dst, bias, heads, out_ch):
            n = x.shape[0]
            xW = (x @ W).reshape(n, heads, out_ch)
            alpha_s = jnp.sum(xW * a_src, axis=-1)
            alpha_d = jnp.sum(xW * a_dst, axis=-1)
            e = jax.nn.leaky_relu(alpha_s[src] + alpha_d[dst], SLOPE)
            m = jax.ops.segment_max(e, dst, num_segments=n)
            w = jnp.exp(e - m[dst])
            z = jax.ops.segment_sum(w, dst, num_segments=n)
            alpha = w / z[dst]
            out = jax.ops.segment_sum(xW[src] * alpha[:, :, None], dst, num_segments=n)
            return out.reshape(n, heads * out_ch) + bias
        loop = jnp.arange(N)
        src = jnp.concatenate([edge_index[0], loop])
        dst = jnp.concatenate([edge_index[1], loop])
        h = jax.nn.elu(gat_layer(x, src, dst, W1, a_src1, a_dst1, b1, H, C))
        return gat_layer(h, src, dst, W2, a_src2, a_dst2, b2, 1, F_DIM)

    def _L3_mix_ref(x, Wq, Wk, Wv, Wm, W1, W2, g1, b1, g2, b2):
        import jax, jax.numpy as jnp
        import numpy as np
        NHEAD = 8
        ATT_EPS = 1e-06
        LN_EPS = 1e-05

        def _layernorm(x, g, b):
            mu = jnp.mean(x, axis=-1, keepdims=True)
            var = jnp.mean(jnp.square(x - mu), axis=-1, keepdims=True)
            return (x - mu) * jax.lax.rsqrt(var + LN_EPS) * g + b
        N, L, C = x.shape
        H = NHEAD
        D = C // H
        q = (x @ Wq).reshape(N, L, H, D)
        k = (x @ Wk).reshape(N, L, H, D)
        v = (x @ Wv).reshape(N, L, H, D)
        Q = jax.nn.elu(q) + 1.0
        K = jax.nn.elu(k) + 1.0
        v = v / L
        KV = jnp.einsum('nshd,nshv->nhdv', K, v)
        Z = 1.0 / (jnp.einsum('nlhd,nhd->nlh', Q, K.sum(axis=1)) + ATT_EPS)
        msg = jnp.einsum('nlhd,nhdv,nlh->nlhv', Q, KV, Z) * L
        msg = msg.reshape(N, L, C) @ Wm
        msg = _layernorm(msg, g1, b1)
        h = jnp.concatenate([x, msg], axis=-1) @ W1
        h = jax.nn.relu(h) @ W2
        msg = _layernorm(h, g2, b2)
        return x + msg

    def _L3_ffn_ref(h, gate_w, gate_b, w1, b1, w2, b2):
        import math
        import jax, jax.numpy as jnp
        import numpy as np
        CAPACITY_FACTOR = 1.25
        B, L, D = h.shape
        E = gate_w.shape[1]
        T = B * L
        C = max(1, math.ceil(CAPACITY_FACTOR * T / E))
        x = h.reshape(T, D)
        logits = x @ gate_w + gate_b
        probs = jax.nn.softmax(logits, axis=-1)
        idx = jnp.argmax(probs, axis=-1)
        prb = jnp.take_along_axis(probs, idx[:, None], axis=1)[:, 0]
        one_hot = jax.nn.one_hot(idx, E, dtype=jnp.float32)
        pos = (jnp.cumsum(one_hot, axis=0) * one_hot).sum(-1).astype(jnp.int32) - 1
        kept = pos < C
        pos_safe = jnp.where(kept, pos, C)
        buf = jnp.zeros((E, C, D), dtype=h.dtype).at[idx, pos_safe].set(x, mode='drop')
        hmid = jax.nn.relu(jnp.einsum('ecd,edf->ecf', buf, w1) + b1[:, None, :])
        ybuf = jnp.einsum('ecf,efd->ecd', hmid, w2) + b2[:, None, :]
        pos_g = jnp.minimum(pos, C - 1)
        y_tok = ybuf[idx, pos_g] * (prb * kept)[:, None]
        y = y_tok.reshape(B, L, D)
        y = jnp.nan_to_num(y, nan=0.0, posinf=10000.0, neginf=-10000.0)
        return y
    edge_index = jnp.stack([src, dst])
    xn = _layernorm(x, axis=-1)
    x = x + _L0_gnn_ref(xn, edge_index, edge_attr_2, L0_gnn_W_forward, L0_gnn_W_reverse, L0_gnn_attn_forward) + _L0_mix_ref(xn[None], L0_mix_Wq, L0_mix_Wkv, L0_mix_Wproj, L0_mix_bproj)[0]
    x = x + _L0_ffn_ref(_layernorm(x, axis=-1)[None], L0_ffn_router_w1, L0_ffn_router_b1, L0_ffn_router_w2, L0_ffn_router_b2, L0_ffn_expert_w1, L0_ffn_expert_b1, L0_ffn_expert_w2, L0_ffn_expert_b2, L0_ffn_expert_w3, L0_ffn_expert_b3)[0]
    xn = _layernorm(x, axis=-1)
    x = x + _L1_gnn_ref(xn, src, dst, L1_gnn_Wq, L1_gnn_bq, L1_gnn_Wk, L1_gnn_bk, L1_gnn_Wv, L1_gnn_bv, L1_gnn_Wo, L1_gnn_bo) + _L1_mix_ref(xn[None], L1_mix_W_qkv, L1_mix_W_out, L1_mix_b_out)[0]
    x = x + _L1_ffn_ref(_layernorm(x, axis=-1)[None], L1_ffn_attention_mask, L1_ffn_wr, L1_ffn_br, L1_ffn_w1, L1_ffn_b1, L1_ffn_w2, L1_ffn_b2)[0]
    xn = _layernorm(x, axis=-1)
    x = x + _L2_gnn_ref(xn, src, dst, edge_type_2, L2_gnn_W_rel, L2_gnn_b_rel, L2_gnn_W_ih, L2_gnn_b_ih, L2_gnn_b_hh, L2_gnn_W1, L2_gnn_b1, L2_gnn_W2, L2_gnn_b2, L2_gnn_W3, L2_gnn_b3) + _L2_mix_ref(xn[None], L2_mix_Wqkv, L2_mix_Wout, L2_mix_gamma)[0]
    x = x + _L2_ffn_ref(_layernorm(x, axis=-1)[None], L2_ffn_router_w, L2_ffn_w1, L2_ffn_b1, L2_ffn_w2, L2_ffn_b2)[0]
    xn = _layernorm(x, axis=-1)
    x = x + _L3_gnn_ref(xn, edge_index, L3_gnn_W1, L3_gnn_a_src1, L3_gnn_a_dst1, L3_gnn_b1, L3_gnn_W2, L3_gnn_a_src2, L3_gnn_a_dst2, L3_gnn_b2) + _L3_mix_ref(xn[None], L3_mix_Wq, L3_mix_Wk, L3_mix_Wv, L3_mix_Wm, L3_mix_W1, L3_mix_W2, L3_mix_g1, L3_mix_b1, L3_mix_g2, L3_mix_b2)[0]
    x = x + _L3_ffn_ref(_layernorm(x, axis=-1)[None], L3_ffn_gate_w, L3_ffn_gate_b, L3_ffn_w1, L3_ffn_b1, L3_ffn_w2, L3_ffn_b2)[0]
    return x

_drawn_inputs = setup_inputs


def setup_inputs(seed=0):
    import zlib

    import numpy as np

    out = dict(_drawn_inputs(seed))
    spreads = {'L0_mix_bproj': (0.0, 0.1),
     'L0_ffn_router_b1': (0.0, 0.1),
     'L0_ffn_router_b2': (0.0, 0.1),
     'L0_ffn_expert_b1': (0.0, 0.443),
     'L0_ffn_expert_b2': (0.0, 0.1),
     'L0_ffn_expert_b3': (0.0, 0.1),
     'L1_mix_b_out': (0.0, 0.1),
     'L1_ffn_b1': (0.0, 0.8),
     'L1_ffn_b2': (0.0, 0.409),
     'L2_mix_gamma': (1.0, 0.2),
     'L2_ffn_b1': (0.0, 0.557),
     'L2_ffn_b2': (0.0, 0.345),
     'L3_gnn_b1': (0.0, 0.5),
     'L3_gnn_b2': (0.0, 0.362),
     'L3_mix_g1': (1.0, 0.554),
     'L3_mix_b1': (0.0, 0.523),
     'L3_mix_g2': (1.0, 0.2),
     'L3_mix_b2': (0.0, 0.356),
     'L3_ffn_gate_b': (0.0, 0.505),
     'L3_ffn_b1': (0.0, 2.0),
     'L3_ffn_b2': (0.0, 2.0)}
    factors = {'L0_mix_Wq': 8.0,
     'L0_mix_Wkv': 6.975,
     'L0_mix_Wproj': 6.721,
     'L1_gnn_Wq': 8.0,
     'L1_gnn_bq': 29.923,
     'L1_gnn_Wk': 8.0,
     'L1_gnn_bk': 200.0,
     'L1_gnn_bv': 3.975,
     'L1_ffn_wr': 3.959,
     'L1_ffn_w1': 4.882,
     'L1_ffn_w2': 3.823,
     'L2_gnn_b_rel': 4.159,
     'L2_gnn_b_ih': 33.428,
     'L2_gnn_b_hh': 34.154,
     'L2_gnn_b1': 3.238,
     'L3_gnn_a_src1': 23.925,
     'L3_gnn_a_dst1': 200.0,
     'L3_gnn_a_src2': 53.392,
     'L3_gnn_a_dst2': 200.0,
     'L3_mix_Wq': 196.459,
     'L3_mix_Wk': 103.473,
     'L3_ffn_w1': 2.795}
    for name, (base, spread) in spreads.items():
        noise = np.random.default_rng([zlib.crc32(name.encode()), seed]).standard_normal(out[name].shape)
        drawn = base * np.exp(spread * noise) if base else spread * noise
        out[name] = jnp.asarray(drawn.astype(out[name].dtype))
    for name, factor in factors.items():
        out[name] = (out[name] * factor).astype(out[name].dtype)
    return out
```

```python
from contextlib import ExitStack, contextmanager

import numpy as np

import concourse.bass as bass
from concourse import mybir

F32 = mybir.dt.float32
BF16 = mybir.dt.bfloat16
I32 = mybir.dt.int32
U32 = mybir.dt.uint32
ALU = mybir.AluOpType
ACT = mybir.ActivationFunctionType
X = mybir.AxisListType.X
DVE_ONLY = [mybir.EngineType.DVE]
ds = bass.ds

P = 128
N = 3125
NT = -(-N // P)
NP = NT * P
PAIRS = NT // 2
LAST = N - (NT - 1) * P
D = 256
CW = 400
NC = NP // CW
E = 50000
SU = 16
ET = -(-E // (125 * SU)) * SU
EFULL = E // ET
DUMP = (P - EFULL) * ET
SB = 8
ST = -(-(E // P + NT) // (2 * SB)) * 2 * SB
NSLOT = ST * P
REC = 8
R_LO, R_KEY, R_OTHER, R_REL, R_D0, R_D1 = range(6)
BIG = 1e30


class Chain:

    def __init__(self, eng, sem):
        self.eng, self.sem, self.base, self.k = eng, sem, 0, 0

    def __call__(self, ins, meanwhile=None):
        self.k += 1
        ins.then_inc(self.sem, 1)
        if meanwhile:
            meanwhile()
        self.eng.wait_ge(self.sem, self.base + self.k)

    @contextmanager
    def loop(self, count, per):
        start = self.base + self.k
        with self.eng.Fori(0, count) as i:
            self.base, self.k = (i * per + start if per else start), 0
            yield i
            assert self.k == per, f"the turn links {self.k} instructions, not {per}"
        self.base, self.k = start + count * per, 0


class Kit:

    def __init__(self, nc, dram):
        self.nc, self.dram, self.loads = nc, dram, 0


class Stage:

    def __init__(self, kit, name):
        self.kit, self.nc, self.name = kit, kit.nc, name
        self.ctx, self.sems = ExitStack(), []

    def __enter__(self):
        return self

    def sb(self, name, shape, dt=F32):
        return self.ctx.enter_context(self.nc.sbuf_tensor(f"{self.name}_{name}", shape, dt))

    def ps(self, name, shape, dt=F32):
        return self.ctx.enter_context(self.nc.psum_tensor(f"{self.name}_{name}", shape, dt))

    def sem(self, name):
        s = self.nc.alloc_semaphore(f"{self.name}_{name}")
        self.sems.append(s)
        return s

    def __exit__(self, *e):
        if e[0] is None:
            self.nc.clear_and_free_semaphores(self.sems)
            self.nc.all_engine_barrier()
        self.ctx.close()


def bcast(ap, n, at):
    shape = list(ap.shape)
    shape.insert(at, n)
    return ap.unsqueeze(at).to_broadcast(shape)


def sort_edges(kit, name, key_dram, other_dram, table, bucket_of_tile):
    nc, dram = kit.nc, kit.dram
    assert EFULL * ET == E and ET % (2 * SB) == 0
    with Stage(kit, name) as s:
        key_i = s.sb("key_i", [P, ET], I32)
        key_f = s.sb("key_f", [P, ET])
        hi_i = s.sb("hi_i", [P, ET], I32)
        hi_f = s.sb("hi_f", [P, ET])
        lo_i = s.sb("lo_i", [P, ET], I32)
        lo_b = s.sb("lo_b", [P, ET])
        key_parts = s.sb("key_parts", [P, 2, ET], BF16)
        other = s.sb("other", [P, ET], I32)
        etype = s.sb("etype", [P, ET], I32)
        attr = s.sb("attr", [P, 2, ET])
        spill = s.sb("spill", [P, ET])
        record = s.sb("record", [P, ET, REC], I32)
        hot_lo = s.sb("hot_lo", [P, ET, P], BF16)
        hot_hi = s.sb("hot_hi", [P, ET, NT], BF16)
        zero_b = s.sb("zero_b", [P, P], BF16)
        ident_b = s.sb("ident_b", [P, P], BF16)
        total = s.sb("total", [P, NT])
        tiles_i = s.sb("tiles_i", [P, NT], I32)
        tiles_f = s.sb("tiles_f", [P, NT])
        after = s.sb("after", [P, NT])
        first = s.sb("first", [P, NT])
        begun = s.sb("begun", [P, NT])
        zeros = s.sb("zeros", [P, NT])
        count = s.sb("count", [P, 2, NT])
        hot_loT = s.sb("hot_loT", [P, 2, P])
        same = s.sb("same", [P, P])
        picked = s.sb("picked", [P, NT])
        base = s.sb("base", [P, ET])
        dup = s.sb("dup", [P, ET])
        pos_i = s.sb("pos_i", [P, ET], I32)
        row_i = s.sb("row_i", [P, ET], I32)
        dest = s.sb("dest", [P, ET], U32)
        dest_now = s.sb("dest_now", [P, 2, SB], U32)
        rec_now = s.sb("rec_now", [P, 2, SB, REC], I32)
        blank = s.sb("blank", [P, 32, REC], I32)
        started = s.sb("started", [P, 16, NT])
        bt = s.sb("bt", [P, ST])
        ps_run = s.ps("ps_run", [P, 512])
        ps_small = s.ps("ps_small", [P, 2, 256])
        ps_loT = s.ps("ps_loT", [P, 2, 1024], BF16)
        ps_key = s.ps("ps_key", [P, 2, 512])
        ps_pick = s.ps("ps_pick", [P, 2, 512])
        loaded = s.sem("loaded")
        cast = s.sem("cast")
        hot = s.sem("hot")
        histogram = s.sem("histogram")
        totals = s.sem("totals")
        prefix = s.sem("prefix")
        based = s.sem("based")
        turned = s.sem("turned")
        counted = s.sem("counted")
        copied = s.sem("copied")
        keyed = s.sem("keyed")
        chosen = s.sem("chosen")
        ranked = s.sem("ranked")
        placed = s.sem("placed")
        blanked = s.sem("blanked")
        blank_set = s.sem("blank_set")
        staged = s.sem("staged")
        scattered = [s.sem(f"scattered{b}") for b in range(2)]
        dve_chain = s.sem("dve_chain")
        recorded = s.sem("recorded")
        gate = s.sb("gate", [P, 2])
        gate_set = s.sem("gate_set")
        rows = table[0:NSLOT, :].rearrange("(p n t) w -> p n t w", p=P, t=32)
        with nc.Block() as block:

            @block.sync
            def _(sp):
                sp.dma_start(key_i[:], key_dram).then_inc(loaded, 16)
                sp.dma_start(other[:], other_dram).then_inc(loaded, 16)
                sp.dma_start(etype[:], dram["edge_type"]).then_inc(loaded, 16)
                sp.dma_start(attr[:], dram["edge_attr"]).then_inc(loaded, 16)
                sp.dma_start(spill[:], dram["spill"]).then_inc(loaded, 16)
                sp.wait_ge(blank_set, 1)
                for n in range(ST // 32):
                    sp.dma_start(rows[:, n], blank[:]).then_inc(blanked, 16)
                sp.wait_ge(blanked, 16 * (ST // 32))
                sp.wait_ge(loaded, 80)

            @block.vector
            def _(dve):
                link = Chain(dve, dve_chain)
                dve.sem_inc(ranked, 4)
                link(nc.vector.memset(zero_b[:], 0.0))
                link(nc.vector.memset(zeros[:], 0.0))
                link(nc.vector.tensor_copy(ident_b[:], kit.ident[:]))
                link(nc.vector.memset(blank[:], 0))
                nc.vector.memset(blank[:, :, R_LO], -1).then_inc(blank_set, 1)
                dve.wait_ge(loaded, 80)
                link(nc.vector.tensor_copy(key_f[:], key_i[:]))
                link(nc.vector.tensor_single_scalar(hi_i[:], key_i[:], 7, ALU.arith_shift_right))
                link(nc.vector.tensor_copy(hi_f[:], hi_i[:]))
                link(nc.vector.scalar_tensor_tensor(out=lo_b[:], in0=hi_f[:], scalar=-float(P), in1=key_f[:],
                                                    op0=ALU.mult, op1=ALU.add))
                link(nc.vector.tensor_copy(key_parts[:, 0, :], lo_b[:]))
                link(nc.vector.tensor_scalar(key_parts[:, 1, :], hi_f[:], float(P), None, ALU.mult))
                nc.vector.tensor_tensor(hot_hi[:], bcast(hi_f[:], NT, 2), bcast(kit.iota[:, 0:NT], ET, 1),
                                        ALU.is_equal).then_inc(cast, 1)
                with dve.Fori(0, ET // SU) as i:
                    nc.vector.tensor_tensor(hot_lo[:, ds(i * SU, SU), :], bcast(lo_b[:, ds(i * SU, SU)], P, 2),
                                            bcast(kit.iota[:], SU, 1), ALU.is_equal).then_inc(hot, 1)
                link(nc.vector.memset(record[:], 0))
                link(nc.vector.tensor_copy(lo_i[:], lo_b[:]))
                nc.vector.tensor_copy(record[:, :, R_LO], lo_i[:]).then_inc(recorded, 1)
                nc.vector.tensor_copy(record[:, :, R_KEY], key_i[:]).then_inc(recorded, 1)
                nc.vector.tensor_copy(record[:, :, R_OTHER], other[:]).then_inc(recorded, 1)
                nc.vector.scalar_tensor_tensor(out=record[:, :, R_REL], in0=etype[:], scalar=float(NP),
                                               in1=other[:], op0=ALU.mult, op1=ALU.add).then_inc(recorded, 1)
                for j, w in enumerate((R_D0, R_D1)):
                    nc.vector.tensor_copy(record[:, :, w].bitcast(F32), attr[:, j, :]).then_inc(recorded, 1)
                dve.wait_ge(histogram, 1)
                nc.vector.tensor_copy(total[:], ps_run[:, 0:NT]).then_inc(totals, 1)
                dve.wait_ge(prefix, 1)
                link(nc.vector.tensor_scalar(tiles_i[:], ps_small[:, 0, 0:NT], float(P - 1), None, ALU.add))
                link(nc.vector.tensor_single_scalar(tiles_i[:], tiles_i[:], 7, ALU.arith_shift_right))
                link(nc.vector.tensor_scalar(tiles_f[:], tiles_i[:], 1.0, None, ALU.max))
                link(nc.vector.tensor_tensor_scan(after[:], zeros[:], tiles_f[:], 0.0, ALU.add, ALU.add))
                link(nc.vector.tensor_tensor(first[:], after[:], tiles_f[:], ALU.subtract))
                nc.vector.scalar_tensor_tensor(out=begun[:], in0=first[:], scalar=float(P), in1=ps_small[:, 1, 0:NT],
                                               op0=ALU.mult, op1=ALU.add).then_inc(based, 1)
                with link.loop(ST // 16, 2) as i:
                    link(nc.vector.tensor_tensor(started[:], bcast(kit.tile_no[:, ds(i * 16, 16)], NT, 2),
                                                 bcast(first[:], 16, 1), ALU.is_ge))
                    dve.wait_ge(based, 1)
                    link(nc.vector.tensor_reduce(bt[:, ds(i * 16, 16)], started[:], X, ALU.add))
                link(nc.vector.tensor_scalar(bucket_of_tile[:], bt[0:1, :], -1.0, None, ALU.add))
                with link.loop(ET // SU, 5) as i:
                    for u in range(SU):
                        t = i * SU + u
                        dve.wait_ge(keyed, t + 1)
                        nc.vector.scalar_tensor_tensor(out=same[:], in0=ps_key[:, u % 2, 0:P], scalar=key_f[:, ds(t, 1)],
                                                       in1=kit.earlier[:], op0=ALU.is_equal, op1=ALU.mult,
                                                       accum_out=dup[:, ds(t, 1)]).then_inc(ranked, 1)
                        dve.wait_ge(chosen, t + 3)
                        nc.vector.scalar_tensor_tensor(out=picked[:], in0=ps_pick[:, u % 2, 0:NT], scalar=1.0,
                                                       in1=hot_hi[:, ds(t, 1), :].squeeze(1), op0=ALU.mult,
                                                       op1=ALU.mult, accum_out=base[:, ds(t, 1)]).then_inc(ranked, 1)
                        dve.wait_ge(ranked, 2 * t + 6)
                    pos, row, bas, to = (x[:, ds(i * SU, SU)] for x in (pos_i, row_i, base, dest))
                    link(nc.vector.tensor_tensor(pos, bas, dup[:, ds(i * SU, SU)], ALU.add))
                    link(nc.vector.tensor_single_scalar(row, pos, P - 1, ALU.bitwise_and))
                    link(nc.vector.tensor_single_scalar(pos, pos, 7, ALU.arith_shift_right))
                    link(nc.vector.scalar_tensor_tensor(out=bas, in0=row, scalar=float(ST), in1=pos,
                                                        op0=ALU.mult, op1=ALU.add))
                    link(nc.vector.scalar_tensor_tensor(out=bas, in0=hi_f[:, ds(i * SU, SU)], scalar=0.0, in1=bas,
                                                        op0=ALU.is_ge, op1=ALU.mult))
                    nc.vector.tensor_tensor(to, bas, spill[:, ds(i * SU, SU)], ALU.add).then_inc(placed, 1)

            @block.tensor
            def _(pe):
                def turn(t, u):
                    pe.wait_ge(copied, 2 * t + 2)
                    nc.tensor.transpose(ps_loT[:, u % 2, 0:P], hot_lo[:, ds(t, 1), :].squeeze(1),
                                        ident_b[:]).then_inc(turned, 1)

                pe.sem_inc(chosen, 2)
                pe.wait_ge(cast, 1)
                nc.tensor.matmul(ps_run[:, 0:NT], zero_b[:], hot_hi[:, 0, :], start=True, stop=True)
                with pe.Fori(0, ET // SU) as i:
                    for u in range(SU):
                        pe.wait_ge(hot, i + 1)
                        nc.tensor.matmul(ps_run[:, 0:NT], hot_lo[:, ds(i * SU + u, 1), :].squeeze(1),
                                         hot_hi[:, ds(i * SU + u, 1), :].squeeze(1), start=False, stop=True,
                                         skip_group_check=True)
                nc.tensor.matmul(ps_run[:, 0:NT], zero_b[:], hot_hi[:, 0, :], start=False, stop=True,
                                 skip_group_check=True).then_inc(histogram, 1)
                pe.wait_ge(totals, 1)
                nc.tensor.matmul(ps_small[:, 0, 0:NT], kit.ones[:], total[:], start=True, stop=True)
                nc.tensor.matmul(ps_small[:, 1, 0:NT], kit.later[:], total[:], start=True,
                                 stop=True).then_inc(prefix, 1)
                pe.wait_ge(based, 1)
                nc.tensor.matmul(ps_run[:, 0:NT], kit.ident[:], begun[:], start=True, stop=True).then_inc(counted, 1)
                with pe.Fori(0, ET // SU) as i:
                    for u in range(SU):
                        t = i * SU + u
                        if u == 0:
                            turn(t, u)
                        pe.wait_ge(ranked, 2 * t + 2)
                        nc.tensor.matmul(ps_key[:, u % 2, 0:P], key_parts[:, 0, ds(t, 1)].to_broadcast([P, P]),
                                         ident_b[:], start=True, stop=False)
                        nc.tensor.matmul(ps_key[:, u % 2, 0:P], key_parts[:, 1, ds(t, 1)].to_broadcast([P, P]),
                                         ident_b[:], start=False, stop=True).then_inc(keyed, 1)
                        if u < SU - 1:
                            turn(t + 1, u + 1)
                        pe.wait_ge(copied, 2 * t + 6)
                        nc.tensor.matmul(ps_run[:, 0:NT], hot_lo[:, ds(t, 1), :].squeeze(1),
                                         hot_hi[:, ds(t, 1), :].squeeze(1), start=False, stop=True,
                                         skip_group_check=True).then_inc(counted, 1)
                        nc.tensor.matmul(ps_pick[:, u % 2, 0:NT], hot_loT[:, u % 2, :], count[:, u % 2, :],
                                         start=True, stop=True).then_inc(chosen, 1)

            @block.scalar
            def _(act):
                act.sem_inc(copied, 4)
                with act.Fori(0, ET // SU) as i:
                    for u in range(SU):
                        t = i * SU + u
                        act.wait_ge(chosen, t + 1)
                        act.wait_ge(turned, t + 1)
                        nc.scalar.copy(hot_loT[:, u % 2, :], ps_loT[:, u % 2, 0:P]).then_inc(copied, 1)
                        act.wait_ge(counted, t + 1)
                        nc.scalar.copy(count[:, u % 2, :], ps_run[:, 0:NT]).then_inc(copied, 1)

            @block.gpsimd
            def _(pool):
                pool.wait_ge(recorded, 6)
                nc.gpsimd.memset(gate[:], 0.0).then_inc(gate_set, 1)
                pool.wait_ge(gate_set, 1)
                pool.wait_ge(blanked, 16 * (ST // 32))
                with pool.Fori(0, ET // (2 * SB)) as i:
                    for b in range(2):
                        t = i * 2 * SB + b * SB
                        pool.wait_ge(placed, i + 1)
                        nc.gpsimd.tensor_copy(dest_now[:, b, :], dest[:, ds(t, SB)]).then_inc(staged, 1)
                        nc.gpsimd.tensor_copy(rec_now[:, b], record[:, ds(t, SB), :]).then_inc(staged, 1)
                        pool.wait_ge(staged, i * 4 + (2 * b + 2))
                        nc.gpsimd.tensor_tensor(gate[:, 0:1], gate[:, 1:2], gate[:, 1:2], ALU.add)
                        for k in range(SB):
                            pool.indirect_dma_start(
                                table, bass.IndirectOffsetOnAxis(dest_now[:, b, k:k + 1], 0),
                                rec_now[:, b, k, :], None).then_inc(scattered[b], 16)
                    for b in range(2):
                        pool.wait_ge(scattered[b], (i + 1) * (16 * SB))


def edge_pass(kit, name, kind, slots, buckets, row_table, row_field, key_table, heads, width, acc, mx):
    nc = kit.nc
    H, V = heads, width
    F = H * V
    soft = kind != "sum"
    two = key_table is not None
    RW = row_table.shape[1]
    M = F + H if soft else F
    R = SB * H
    turns = ST // (2 * SB)
    per_batch = 2 if soft else 1

    def scale_on_act(q):
        return H == 1

    weigh_on_act = soft and H <= 4

    links = 2 * (5 + 2 * 7 + 8 * (1 if H == 1 else 2) + {"sum": 0, "dot": 1, "add": 1, "dual": 3}[kind])
    with Stage(kit, name) as s:
        rec = s.sb("rec", [P, ST, REC], I32)
        lo = s.sb("lo", [P, ST])
        row_of = s.sb("row_of", [P, ST], U32)
        row_now = s.sb("row_now", [P, 2, SB], U32)
        rows = s.sb("rows", [P, 2, SB, RW])
        gate = s.sb("gate", [P, 2])
        hot = s.sb("hot", [P, SB, P])
        if two:
            KW = key_table.shape[1]
            key_of = s.sb("key_of", [P, ST], U32)
            key_now = s.sb("key_now", [P, 2, SB], U32)
            keyrows = s.sb("keyrows", [P, 2, SB, KW])
        if kind == "dot":
            prod = s.sb("prod", [P, SB, KW])
        if kind == "dual":
            half = RW // 2
            msg = s.sb("msg", [P, SB, half])
            msg2 = s.sb("msg2", [P, SB, half])
            d01 = s.sb("d01", [P, 2, ST])
        if soft:
            score_all = s.sb("score", [P, P])
            score_now = score_all[:, 0:R].rearrange("p (k h) -> p k h", k=SB)
            lo_h_all = s.sb("lo_h", [P, P])
            lo_h = lo_h_all[:, 0:R].rearrange("p (k h) -> p k h", k=SB)
            loT = s.sb("loT", [R, P])
            edge = s.sb("edge", [R, P + 1])
            wall = s.sb("wall", [R, P + 1])
            runs = s.sb("runs", [R, 2, P])
            top = s.sb("top", [P, 2, P])
            shifted = s.sb("shifted", [P, SB, H])
            weight = s.sb("weight", [P, SB, H])
            rhs = s.sb("rhs", [P, SB, M])
            absent = s.sb("absent", [P, 4, H])
            tile_max = s.sb("tile_max", [P, 4, H])
            new_max = s.sb("new_max", [P, 4, H])
            fall = s.sb("fall", [P, 4, 2, H])
            factor = s.sb("factor", [P, 4, 2, H])
            old_max = s.sb("old_max", [P, 4, H])
            part = (prod[:].rearrange("p k w -> p (k w)")[:, 0:4 * F].rearrange("p (k f) -> p k f", k=4)
                    if kind == "dot" else s.sb("part", [P, 4, F])[:])
            ps_turn = s.ps("ps_turn", [P, 2, 256])
            ps_back = s.ps("ps_back", [P, 2, 256])
        ps_sum = s.ps("ps_sum", [P, 4, 512])
        loaded = s.sem("loaded")
        ready = s.sem("ready")
        staged = s.sem("staged")
        gate_set = s.sem("gate_set")
        gathered = [s.sem(f"gathered{b}") for b in range(2)]
        freed = s.sem("freed")
        scored = s.sem("scored")
        turned = s.sem("turned")
        maxed = s.sem("maxed")
        returned = s.sem("returned")
        lowered = s.sem("lowered")
        weighted = s.sem("weighted")
        weighed = s.sem("weighed")
        listed = s.sem("listed")
        summed = s.sem("summed")
        merged = s.sem("merged")
        falls = s.sem("falls")
        factors = s.sem("factors")
        chain = s.sem("chain")
        with nc.Block() as block:

            @block.sync
            def _(sp):
                sp.dma_start(rec[:], slots[0:NSLOT, :].rearrange("(p t) w -> p t w", p=P)).then_inc(loaded, 16)
                sp.wait_ge(loaded, 16)

            @block.gpsimd
            def _(pool):
                nc.gpsimd.memset(gate[:], 0.0).then_inc(gate_set, 1)
                pool.wait_ge(gate_set, 1)
                pool.wait_ge(ready, 1)
                copies = 2 if two else 1
                with pool.Fori(0, turns) as i:
                    for b in range(2):
                        n = i * 2 + b
                        pool.wait_ge(freed, n * per_batch + per_batch)
                        pool.wait_ge(ready, 1)
                        nc.gpsimd.tensor_copy(row_now[:, b, :], row_of[:, ds(n * SB, SB)]).then_inc(staged, 1)
                        if two:
                            nc.gpsimd.tensor_copy(key_now[:, b, :], key_of[:, ds(n * SB, SB)]).then_inc(staged, 1)
                        pool.wait_ge(staged, (n + 1) * copies)
                        nc.gpsimd.tensor_tensor(gate[:, 0:1], gate[:, 1:2], gate[:, 1:2], ALU.add)
                        for k in range(SB):
                            pool.indirect_dma_start(rows[:, b, k, :], None, row_table, bass.IndirectOffsetOnAxis(
                                row_now[:, b, k:k + 1], 0)).then_inc(gathered[b], 16)
                            if two:
                                pool.indirect_dma_start(keyrows[:, b, k, :], None, key_table, bass.IndirectOffsetOnAxis(
                                    key_now[:, b, k:k + 1], 0)).then_inc(gathered[b], 16)

            @block.vector
            def _(dve):
                link = Chain(dve, chain)
                dve.wait_ge(loaded, 16)
                link(nc.vector.tensor_copy(lo[:], rec[:, :, R_LO]))
                if two:
                    link(nc.vector.tensor_copy(key_of[:], rec[:, :, R_KEY].bitcast(U32)))
                if kind == "dual":
                    for j, w in enumerate((R_D0, R_D1)):
                        link(nc.vector.tensor_copy(d01[:, j, :], rec[:, :, w].bitcast(F32)))
                if soft:
                    link(nc.vector.memset(edge[:], 1.0))
                    for b in (score_all, lo_h_all, top):
                        link(nc.vector.memset(b[:], 0.0))
                    link(nc.vector.memset(mx[:], -BIG))
                link(nc.vector.memset(acc[:], 0.0))
                if not weigh_on_act:
                    dve.sem_inc(freed, 2 * per_batch)
                dve.sem_inc(merged, 1 if soft else 4)
                nc.vector.tensor_copy(row_of[:], rec[:, :, row_field].bitcast(U32)).then_inc(ready, 1)

                def bucket_registers(n):
                    return nc.values_load_multi_w_load_instructions(
                        buckets[:, ds(n * SB, SB)], engines=DVE_ONLY, min_val=0, max_val=NT - 1,
                        skip_runtime_bounds_check_because="a count of 1 to NT buckets begun, less one")[1]

                def scores(b, n, meanwhile):
                    g = rows[:, b]
                    if kind == "dot":
                        link(nc.vector.tensor_tensor(prod[:], g[:, :, 0:KW], keyrows[:, b], ALU.mult), meanwhile)
                        nc.vector.tensor_reduce(score_now.rearrange("p k h -> p (k h)"),
                                                prod[:].rearrange("p k (h v) -> p (k h) v", h=H), X, ALU.add)
                    if kind == "add":
                        link(nc.vector.tensor_tensor(score_now, g[:, :, F:F + H], keyrows[:, b], ALU.add), meanwhile)
                        nc.vector.scalar_tensor_tensor(out=score_now, in0=score_now, scalar=0.2, in1=score_now,
                                                       op0=ALU.mult, op1=ALU.max)
                    if kind == "dual":
                        nc.vector.tensor_tensor(msg[:], g[:, :, 0:half],
                                                bcast(d01[:, 0, ds(n * SB, SB)], half, 2), ALU.mult)
                        link(nc.vector.tensor_tensor(msg2[:], g[:, :, half:RW],
                                                     bcast(d01[:, 1, ds(n * SB, SB)], half, 2), ALU.mult), meanwhile)
                        link(nc.vector.tensor_tensor(msg[:], msg[:], msg2[:], ALU.add))
                        link(nc.vector.scalar_tensor_tensor(out=score_now, in0=msg[:, :, V - 1:half], scalar=0.2,
                                                            in1=msg[:, :, V - 1:half], op0=ALU.mult, op1=ALU.max))
                        nc.vector.memset(msg[:, :, V - 1], 1.0)

                if not soft:
                    with link.loop(turns, 0) as i:
                        for b in range(2):
                            n = i * 2 + b
                            r = bucket_registers(n)
                            dve.wait_ge(gathered[b], (i + 1) * (16 * SB))
                            nc.vector.tensor_tensor(hot[:], bcast(kit.iota[:], SB, 1), bcast(lo[:, ds(n * SB, SB)], P, 2),
                                                    ALU.is_equal).then_inc(weighed, 1)
                            for k in range(SB):
                                dve.wait_ge(summed, n * SB + (k + 1))
                                a = acc[:, ds(r[k], 1), :].squeeze(1)
                                nc.vector.tensor_tensor(a, ps_sum[:, k % 4, 0:F], a, ALU.add).then_inc(merged, 1)
                                dve.wait_ge(merged, n * SB + (k + 5))
                            dve.sem_inc(freed, 1)
                    return

                def score(b, t, n, meanwhile=None):
                    dve.wait_ge(gathered[b], (t + 1) * (16 * SB * (2 if two else 1)))
                    if kind == "dual":
                        dve.wait_ge(freed, n * 2 + 4)
                    if not isinstance(n, int) or n > 0:
                        dve.wait_ge(lowered, n)
                    scores(b, n, meanwhile)
                    nc.vector.tensor_scalar(lo_h, bcast(lo[:, ds(n * SB, SB)], H, 2), 0.0, None,
                                            ALU.add).then_inc(scored, 1)

                def segment_maxima(n):
                    dve.wait_ge(turned, n + 1)
                    link(nc.vector.tensor_copy(loT[:], ps_turn[0:R, 1, 0:P]))
                    link(nc.vector.tensor_tensor(edge[:, 1:P], loT[:, 0:P - 1], loT[:, 1:P], ALU.not_equal))
                    link(nc.vector.tensor_scalar(wall[:], edge[:], -BIG, None, ALU.mult))
                    nc.vector.tensor_tensor_scan(runs[:, 0, :], wall[:, 0:P], ps_turn[0:R, 0, 0:P], -BIG,
                                                 ALU.add, ALU.max)
                    link(nc.vector.tensor_tensor_scan(runs[:, 1, ::-1], wall[:, P:0:-1], ps_turn[0:R, 0, 0:P][:, ::-1],
                                                      -BIG, ALU.add, ALU.max))
                    link(nc.vector.tensor_tensor(top[0:R, 0, :], runs[:, 0, :], runs[:, 1, :], ALU.max))
                    nc.vector.tensor_tensor(top[0:R, 1, :], top[0:R, 0, :], edge[:, 1:P + 1],
                                            ALU.mult).then_inc(maxed, 1)

                def lower(n):
                    dve.wait_ge(returned, n + 1)
                    nc.vector.tensor_tensor(shifted[:].rearrange("p k h -> p (k h)"),
                                            score_all[:, 0:R], ps_back[:, 0, 0:R],
                                            ALU.subtract).then_inc(lowered, 1)

                def hot_rows(n, k):
                    nc.vector.tensor_scalar(hot[:, k, :], kit.iota[:], lo[:, ds(n * SB + k, 1)], None, ALU.is_equal)

                def list_maxima():
                    nc.vector.tensor_copy(rhs[:, :, F:M], ps_back[:, 1, 0:R].rearrange("p (k h) -> p k h", k=SB)
                                          ).then_inc(listed, 1)

                def weigh(b, n, tiles):
                    if weigh_on_act:
                        return
                    dve.wait_ge(weighted, n + 1)
                    out = rhs[:, tiles, 0:F].rearrange("p k (h v) -> p k h v", h=H)
                    src = rows[:, b, tiles, KW:RW].rearrange("p k (h v) -> p k h v", h=H)
                    ins = nc.vector.tensor_tensor(out, src, bcast(weight[:, tiles, :], V, 3), ALU.mult)
                    if tiles.stop in (SB // 2, SB):
                        ins.then_inc(freed, 1)

                def each(work, *args):
                    return [lambda k=k: work(*args, k) for k in range(4)]

                def raise_maxima(n, q, r, meanwhile=(None,) * 4):
                    dve.wait_ge(summed, n * SB + (4 * q + 4))
                    z = ps_sum[:, :, 0:F].rearrange("p k (h v) -> p k h v", h=H)[:, :, :, V - 1]
                    link(nc.vector.tensor_scalar(absent[:], z, 0.0, -BIG, ALU.is_equal, ALU.mult))
                    link(nc.vector.tensor_tensor(tile_max[:], ps_sum[:, :, F:M], absent[:], ALU.add))
                    for k in range(4):
                        m = mx[:, ds(r[4 * q + k], 1), :].squeeze(1)
                        nc.vector.tensor_scalar(old_max[:, k, :], m, 0.0, None, ALU.add)
                        link(nc.vector.tensor_tensor(m, m, tile_max[:, k, :], ALU.max), meanwhile[k])
                    link(nc.vector.tensor_tensor(new_max[:], old_max[:], tile_max[:], ALU.max))
                    nc.vector.tensor_tensor(fall[:, :, 0, :], old_max[:], new_max[:], ALU.subtract)
                    nc.vector.tensor_tensor(fall[:, :, 1, :], tile_max[:], new_max[:],
                                            ALU.subtract).then_inc(falls, 1)

                def merge(n, q, r, meanwhile=(None,) * 4):
                    if scale_on_act(q):
                        dve.wait_ge(merged, n * 2 + (q + 2))
                    else:
                        dve.wait_ge(factors, n * 2 + (q + 1))
                        nc.vector.tensor_tensor(part.rearrange("p k (h v) -> p k h v", h=H),
                                                ps_sum[:, :, 0:F].rearrange("p k (h v) -> p k h v", h=H),
                                                bcast(factor[:, :, 1, :], V, 3), ALU.mult).then_inc(merged, 1)
                        dve.wait_ge(merged, n * 2 + (q + 2))
                    for k in range(4):
                        a = acc[:, ds(r[4 * q + k], 1), :].squeeze(1)
                        if H == 1:
                            link(nc.vector.scalar_tensor_tensor(out=a, in0=a, scalar=factor[:, k, 0, 0:1],
                                                                in1=part[:, k, :], op0=ALU.mult, op1=ALU.add),
                                 meanwhile[k])
                        else:
                            ah = a.rearrange("p (h v) -> p h v", h=H)
                            link(nc.vector.tensor_tensor(ah, ah, bcast(factor[:, k, 0, :], V, 2), ALU.mult))
                            link(nc.vector.tensor_tensor(a, a, part[:, k, :], ALU.add), meanwhile[k])

                def step(n, nxt):
                    if not nxt:
                        r = bucket_registers(n)
                        for q in range(2):
                            raise_maxima(n, q, r)
                            merge(n, q, r)
                        return
                    n1, b1, t1 = nxt
                    r = []
                    score(b1, t1, n1, lambda: r.extend(bucket_registers(n)))
                    raise_maxima(n, 0, r)
                    segment_maxima(n1)
                    merge(n, 0, r, each(lambda k: hot_rows(n1, k)))
                    lower(n1)
                    raise_maxima(n, 1, r, each(lambda k: hot_rows(n1, 4 + k)))
                    list_maxima()
                    weigh(b1, n1, slice(0, 4))
                    if weigh_on_act:
                        merge(n, 1, r)
                    else:
                        merge(n, 1, r, each(lambda k: weigh(b1, n1, slice(4 + k, 5 + k))))

                score(0, 0, 0)
                segment_maxima(0)
                lower(0)
                for k in range(SB):
                    hot_rows(0, k)
                list_maxima()
                weigh(0, 0, slice(0, 4))
                weigh(0, 0, slice(4, 8))
                with link.loop(turns - 1, links) as i:
                    step(i * 2, (i * 2 + 1, 1, i))
                    step(i * 2 + 1, (i * 2 + 2, 0, i + 1))
                step(2 * turns - 2, (2 * turns - 1, 1, turns - 1))
                step(2 * turns - 1, None)

            @block.tensor
            def _(pe):
                if not soft:
                    with pe.Fori(0, turns) as i:
                        for b in range(2):
                            n = i * 2 + b
                            for k in range(SB):
                                if k % 4 == 0:
                                    pe.wait_ge(weighed, n + 1)
                                pe.wait_ge(merged, n * SB + (k + 1))
                                nc.tensor.matmul(ps_sum[:, k % 4, 0:M], hot[:, k, :], rows[:, b, k, :],
                                                 start=True, stop=True).then_inc(summed, 1)
                    return

                def turn(n):
                    pe.wait_ge(scored, n + 1)
                    nc.tensor.transpose(ps_turn[:, 0, 0:P], score_all[:], kit.ident[:])
                    nc.tensor.transpose(ps_turn[:, 1, 0:P], lo_h_all[:], kit.ident[:]).then_inc(turned, 1)
                    pe.wait_ge(maxed, n + 1)
                    nc.tensor.transpose(ps_back[:, 0, 0:P], top[:, 0, :], kit.ident[:])
                    nc.tensor.transpose(ps_back[:, 1, 0:P], top[:, 1, :], kit.ident[:]).then_inc(returned, 1)

                def sums(n, q):
                    pe.wait_ge(listed, n + 1)
                    pe.wait_ge(freed, n * 2 + (q + 5))
                    pe.wait_ge(merged, n * 2 + (q + 1))
                    for k in range(4):
                        nc.tensor.matmul(ps_sum[:, k, 0:M], hot[:, 4 * q + k, :], rhs[:, 4 * q + k, :],
                                         start=True, stop=True).then_inc(summed, 1)

                turn(0)
                sums(0, 0)
                with pe.Fori(0, turns - 1) as i:
                    for b in range(2):
                        n = i * 2 + (b + 1)
                        turn(n)
                        sums(i * 2 + b, 1)
                        sums(n, 0)
                turn(2 * turns - 1)
                sums(2 * turns - 2, 1)
                sums(2 * turns - 1, 0)
                sums(2 * turns - 1, 1)

            @block.scalar
            def _(act):
                if not soft:
                    return

                def weights(n):
                    act.wait_ge(lowered, n + 1)
                    if weigh_on_act:
                        act.wait_ge(freed, n * 2 + 4)
                    nc.scalar.activation(weight[:], shifted[:], ACT.Exp).then_inc(weighted, 1)

                def weigh(b, n, tiles):
                    if not weigh_on_act:
                        return
                    act.wait_ge(weighted, n + 1)
                    for k in tiles:
                        if k == 4 and not (isinstance(n, int) and n == 0):
                            act.wait_ge(summed, n * SB)
                        for h in range(H):
                            src = msg[:, k, 0:V] if kind == "dual" else rows[:, b, k, h * V:(h + 1) * V]
                            ins = nc.scalar.activation(rhs[:, k, h * V:(h + 1) * V], src, ACT.Copy,
                                                       scale=weight[:, k, h:h + 1])
                        if k % 4 == 3:
                            ins.then_inc(freed, 1)

                def rescale(n, q):
                    act.wait_ge(falls, n * 2 + (q + 1))
                    nc.scalar.activation(factor[:], fall[:], ACT.Exp).then_inc(factors, 1)
                    if scale_on_act(q):
                        act.wait_ge(factors, n * 2 + (q + 1))
                        for k in range(4):
                            for h in range(H):
                                ins = nc.scalar.activation(part[:, k, h * V:(h + 1) * V], ps_sum[:, k, h * V:(h + 1) * V],
                                                           ACT.Copy, scale=factor[:, k, 1, h:h + 1])
                        ins.then_inc(merged, 1)

                if weigh_on_act:
                    act.sem_inc(freed, 2 * per_batch)
                weights(0)
                weigh(0, 0, range(SB))
                early = 4 // H if H <= 4 else 0
                with act.Fori(0, turns - 1) as i:
                    for b in range(2):
                        n = i * 2 + b
                        rescale(n, 0)
                        weights(n + 1)
                        weigh(1 - b, n + 1, range(early))
                        rescale(n, 1)
                        weigh(1 - b, n + 1, range(early, SB))
                n = 2 * turns - 2
                rescale(n, 0)
                weights(n + 1)
                weigh(1, n + 1, range(early))
                rescale(n, 1)
                weigh(1, n + 1, range(early, SB))
                rescale(n + 1, 0)
                rescale(n + 1, 1)


def at(buf, f, c):
    if isinstance(buf, tuple):
        n = buf[0].shape[1]
        return at(buf[0], f, c) if f < n else at(buf[1], f - n, c)
    return buf[:, f, ds(c * CW, CW)] if buf.shape[2] == NP else buf[:, f, :]


def layernorm(kit, name, src, dst, gamma=None, beta=None, add_to=None, plus=None):
    nc = kit.nc
    with Stage(kit, name) as s:
        centred_x = s.sb("centred_x", [P, 2, 2, CW])
        square = s.sb("square", [P, 2, 2, CW])
        root = s.sb("root", [P, 2, CW])
        ps_mean = s.ps("ps_mean", [P, 2, 512])
        ps_var = s.ps("ps_var", [P, 2, 512])
        averaged, centred, squared, spread, rooted, normed, chain = (
            s.sem(n) for n in ("averaged", "centred", "squared", "spread", "rooted", "normed", "chain"))
        per = 2 * (1 + (2 if gamma is not None else 1)) if add_to is not None else 2
        with nc.Block() as block:

            @block.tensor
            def _(pe):
                with pe.Fori(0, NC // 2) as i:
                    for u in range(2):
                        c = i * 2 + u
                        pe.wait_ge(centred, c + 1)
                        for f in range(2):
                            ins = nc.tensor.matmul(ps_mean[:, u, 0:CW], kit.mean[:], src[:, f, ds(c * CW, CW)],
                                                   start=f == 0, stop=f == 1)
                        ins.then_inc(averaged, 1)
                    for u in range(2):
                        pe.wait_ge(squared, i * 2 + (u + 1))
                        for f in range(2):
                            ins = nc.tensor.matmul(ps_var[:, u, 0:CW], kit.mean[:], square[:, u, f, :],
                                                   start=f == 0, stop=f == 1)
                        ins.then_inc(spread, 1)

            @block.scalar
            def _(act):
                with act.Fori(0, NC // 2) as i:
                    for u in range(2):
                        act.wait_ge(centred, i * 2 + (u + 3))
                        nc.scalar.activation(square[:, u], centred_x[:, u], ACT.Square).then_inc(squared, 1)
                    for u in range(2):
                        act.wait_ge(spread, i * 2 + (u + 1))
                        nc.scalar.activation(root[:, u, :], ps_var[:, u, 0:CW], ACT.Sqrt,
                                             bias=kit.eps[:]).then_inc(rooted, 1)

            @block.vector
            def _(dve):
                link = Chain(dve, chain)
                dve.sem_inc(centred, 2)
                with link.loop(NC // 2, per) as i:
                    for u in range(2):
                        c = i * 2 + u
                        dve.wait_ge(averaged, c + 1)
                        nc.vector.tensor_tensor(centred_x[:, u], src[:, :, ds(c * CW, CW)],
                                                bcast(ps_mean[:, u, 0:CW], 2, 1), ALU.subtract).then_inc(centred, 1)
                    for u in range(2):
                        c = i * 2 + u
                        here = (slice(None), slice(None), ds(c * CW, CW))
                        dve.wait_ge(rooted, c + 1)
                        link(nc.vector.reciprocal(root[:, u, :], root[:, u, :]))
                        if add_to is None:
                            nc.vector.tensor_tensor(dst[here], centred_x[:, u], bcast(root[:, u, :], 2, 1),
                                                    ALU.mult).then_inc(normed, 1)
                            dve.wait_ge(normed, c + 1)
                            continue
                        link(nc.vector.tensor_tensor(centred_x[:, u], centred_x[:, u], bcast(root[:, u, :], 2, 1),
                                                     ALU.mult))
                        for f in range(2):
                            to = add_to[:, f, ds(c * CW, CW)]
                            ins = nc.vector.scalar_tensor_tensor(out=to, in0=centred_x[:, u, f, :],
                                                                 scalar=gamma[:, f:f + 1], in1=to,
                                                                 op0=ALU.mult, op1=ALU.add)
                        link(ins)


class Layer:

    def __init__(self, w, src, dst, bias=None, func="linear", add=False, blocks=None, scale=1.0,
                 floor=0.0, plus=0.0, other=None):
        self.floor, self.plus, self.other = floor, plus, other
        self.w, self.src, self.dst, self.bias, self.func, self.add = w, src, dst, bias, func, add
        self.ins = sum(x.shape[1] for x in (src if isinstance(src, tuple) else (src,)))
        self.outs = blocks or w.shape[2] // P
        self.scale = scale
        self.dve = isinstance(func, str)


def bank_free(j, n):
    return j + 1 if j >= 4 else j + 4 * ((n - 1 - j) // 4) + 5 - n


def layers(kit, name, stack, loads=(), last=None):
    nc = kit.nc
    acts = sum(y.outs for y in stack if not y.dve)
    dves = sum(y.outs for y in stack if y.dve)
    elus = sum(y.outs for y in stack if y.func == "elu1")
    linked = sum(y.outs for y in stack if y.func == "reciprocal")
    with Stage(kit, name) as s:
        ps_act = s.ps("ps_act", [P, 4, 512]) if acts else None
        ps_dve = s.ps("ps_dve", [P, 4, 512]) if dves else None
        power = s.sb("power", [P, 2, CW])
        loaded, made_act, taken_act, made_dve, taken_dve, lowered, raised, chain = (
            s.sem(n) for n in ("loaded", "made_act", "taken_act", "made_dve", "taken_dve", "lowered", "raised", "chain"))
        with nc.Block() as block:

            @block.sync
            def _(sp):
                for to, frm in loads:
                    sp.dma_start(to, frm).then_inc(loaded, 16)
                if loads:
                    sp.wait_ge(loaded, 16 * len(loads))

            @block.tensor
            def _(pe):
                if loads:
                    pe.wait_ge(loaded, 16 * len(loads))
                with pe.Fori(0, NC) as c:
                    a = d = 0
                    for y in stack:
                        if y is not stack[0]:
                            if a:
                                pe.wait_ge(taken_act, c * acts + (a + 4))
                            if d:
                                pe.wait_ge(taken_dve, c * dves + (d + 4))
                        for o in range(y.outs):
                            if y.dve:
                                pe.wait_ge(taken_dve, c * dves + bank_free(d, dves))
                                to, made = ps_dve[:, d % 4, 0:CW], made_dve
                                d += 1
                            else:
                                pe.wait_ge(taken_act, c * acts + bank_free(a, acts))
                                to, made = ps_act[:, a % 4, 0:CW], made_act
                                a += 1
                            for f in range(y.ins):
                                ins = nc.tensor.matmul(to, y.w[:, f, o * P:(o + 1) * P], at(y.src, f, c),
                                                       start=f == 0, stop=f == y.ins - 1)
                            ins.then_inc(made, 1)

            @block.scalar
            def _(act):
                act.sem_inc(taken_act, 4)
                if loads:
                    act.wait_ge(loaded, 16 * len(loads))
                if not acts and not elus:
                    return
                with act.Fori(0, NC) as c:
                    a = d = e = 0
                    for y in stack:
                        for o in range(y.outs):
                            if not y.dve:
                                act.wait_ge(made_act, c * acts + (a + 1))
                                nc.scalar.activation(y.dst[:, o, :], ps_act[:, a % 4, 0:CW], y.func,
                                                     bias=y.bias[:, o:o + 1] if y.bias is not None else 0.0,
                                                     scale=y.scale).then_inc(taken_act, 1)
                                a += 1
                            else:
                                d += 1
                                if y.func == "elu1":
                                    act.wait_ge(made_dve, c * dves + d)
                                    if e >= 2:
                                        act.wait_ge(taken_dve, c * dves + (d - 2 + 4))
                                    else:
                                        act.wait_ge(taken_dve, c * dves + 4)
                                    nc.scalar.activation(power[:, e % 2, :], ps_dve[:, (d - 1) % 4, 0:CW], ACT.Relu,
                                                         scale=-1.0).then_inc(lowered, 1)
                                    act.wait_ge(lowered, c * elus + (e + 1))
                                    nc.scalar.activation(power[:, e % 2, :], power[:, e % 2, :], ACT.Exp,
                                                         scale=-1.0).then_inc(raised, 1)
                                    e += 1

            @block.vector
            def _(dve):
                dve.sem_inc(taken_dve, 4)
                if loads:
                    dve.wait_ge(loaded, 16 * len(loads))
                if not dves:
                    return
                link = Chain(dve, chain)
                with link.loop(NC, linked) as c:
                    d = e = 0
                    for y in stack:
                        for o in range(y.outs):
                            if not y.dve:
                                continue
                            got, to = ps_dve[:, d % 4, 0:CW], at(y.dst, o, c)
                            d += 1
                            if y.func == "elu1":
                                dve.wait_ge(raised, c * elus + (e + 1))
                                ins = nc.vector.scalar_tensor_tensor(out=to, in0=got, scalar=0.0, in1=power[:, e % 2, :],
                                                                     op0=ALU.max, op1=ALU.add)
                                e += 1
                            else:
                                dve.wait_ge(made_dve, c * dves + d)
                                b = y.bias[:, o:o + 1] if y.bias is not None else 0.0
                                if y.func == "reciprocal":
                                    link(nc.vector.tensor_scalar(to, got, y.floor, y.plus, ALU.max, ALU.add))
                                    ins = nc.vector.reciprocal(to, to)
                                elif y.func == "times":
                                    ins = nc.vector.scalar_tensor_tensor(out=to, in0=got, scalar=y.scale,
                                                                         in1=at(y.other, o, c), op0=ALU.mult,
                                                                         op1=ALU.mult)
                                elif y.add:
                                    ins = nc.vector.scalar_tensor_tensor(out=to, in0=got, scalar=b, in1=to,
                                                                         op0=ALU.add, op1=ALU.add)
                                elif y.func == "relu":
                                    ins = nc.vector.tensor_scalar(to, got, b, 0.0, ALU.add, ALU.max)
                                else:
                                    ins = nc.vector.tensor_scalar(to, got, b, y.scale, ALU.add, ALU.mult)
                            ins.then_inc(taken_dve, 1)
                            dve.wait_ge(taken_dve, c * dves + (d + 4))


def turn_rows(kit, name, rows, dst, add=False, bias=None):
    nc = kit.nc
    W = min(P, rows.shape[2])
    width = rows.shape[2] // W
    if W < P:
        dst = dst.unsqueeze(1)
    with Stage(kit, name) as s:
        tile = s.sb("tile", [P, 2, width * W])
        ps_t = s.ps("ps_t", [P, 2, 512])
        staged, turned, taken = (s.sem(n) for n in ("staged", "turned", "taken"))
        with nc.Block() as block:

            @block.gpsimd
            def _(pool):
                pool.wait_ge(taken, 1)
                with pool.Fori(0, PAIRS) as i:
                    for u in range(2):
                        t = i * 2 + u
                        pool.wait_ge(turned, t + 1)
                        pool.wait_ge(taken, 1)
                        nc.gpsimd.tensor_copy(tile[:, u, :], rows[:, ds(t, 1), :].squeeze(1)).then_inc(staged, 1)
                pool.wait_ge(turned, 2 * PAIRS + 1)
                nc.gpsimd.tensor_copy(tile[:, 0, :], rows[:, NT - 1, :]).then_inc(staged, 1)

            @block.tensor
            def _(pe):
                pe.sem_inc(turned, 2)

                def one(t, u):
                    pe.wait_ge(taken, t + 1)
                    pe.wait_ge(staged, t + 1)
                    for f in range(width):
                        ins = nc.tensor.transpose(ps_t[0:W, u, f * P:(f + 1) * P], tile[:, u, f * W:(f + 1) * W],
                                                  kit.ident[:])
                    ins.then_inc(turned, 1)

                with pe.Fori(0, PAIRS) as i:
                    for u in range(2):
                        one(i * 2 + u, u)
                one(NT - 1, 0)

            @block.vector
            def _(dve):
                dve.sem_inc(taken, 2)

                def one(t, u):
                    dve.wait_ge(turned, t + 3)
                    for f in range(width):
                        to = dst[:, f, ds(t * P, P)]
                        got = ps_t[0:W, u, f * P:(f + 1) * P]
                        b = bias[:, f:f + 1] if bias is not None else 0.0
                        if add:
                            ins = nc.vector.scalar_tensor_tensor(out=to, in0=got, scalar=b, in1=to, op0=ALU.add,
                                                                 op1=ALU.add)
                        else:
                            ins = nc.vector.tensor_scalar(to, got, b, None, ALU.add)
                    ins.then_inc(taken, 1)

                with dve.Fori(0, PAIRS) as i:
                    for u in range(2):
                        one(i * 2 + u, u)
                one(NT - 1, 0)


def rows_of(kit, name, groups, finish, loads=(), sink=None, links=0, setup=None):
    nc = kit.nc
    srcs = []
    for g in groups:
        if not any(g[0] is x for x in srcs):
            srcs.append(g[0])
    with Stage(kit, name) as s:
        lhs = [s.sb(f"lhs{j}", [P, 2, x.shape[1], P]) for j, x in enumerate(srcs)]
        ps = [s.ps(f"ps{j}", [P, 2, 512]) for j in range(len(groups))]
        loaded, staged, made, taken, chain, set_up = (
            s.sem(n) for n in ("loaded", "staged", "made", "taken", "chain", "set_up"))
        stored = [s.sem(f"stored{u}") for u in range(2)]
        extra = setup(s) if setup else None
        dmas = 16 * (sink(None, None, None, extra) if sink else 0)
        ns = len(srcs)
        with nc.Block() as block:

            @block.sync
            def _(sp):
                for to, frm in loads:
                    sp.dma_start(to, frm).then_inc(loaded, 16)
                if loads:
                    sp.wait_ge(loaded, 16 * len(loads))
                if not sink:
                    return
                for u in range(2):
                    sp.sem_inc(stored[u], dmas)
                with sp.Fori(0, PAIRS) as i:
                    for u in range(2):
                        sp.wait_ge(taken, i * 2 + (u + 3))
                        sink(sp, i * 2 + u, u, extra, stored[u])
                sp.wait_ge(taken, NT + 2)
                sink(sp, NT - 1, 0, extra, stored[0])
                sp.wait_ge(stored[0], dmas * (PAIRS + 2))
                sp.wait_ge(stored[1], dmas * (PAIRS + 1))

            @block.gpsimd
            def _(pool):
                pool.sem_inc(set_up, 1)
                with pool.Fori(0, PAIRS) as i:
                    for u in range(2):
                        t = i * 2 + u
                        pool.wait_ge(made, t + 1)
                        pool.wait_ge(set_up, 1)
                        for j, x in enumerate(srcs):
                            nc.gpsimd.tensor_copy(lhs[j][:, u], x[:, :, ds(t * P, P)]).then_inc(staged, 1)
                pool.wait_ge(made, 2 * PAIRS + 1)
                for j, x in enumerate(srcs):
                    nc.gpsimd.tensor_copy(lhs[j][:, 0], x[:, :, ds((NT - 1) * P, P)]).then_inc(staged, 1)

            @block.tensor
            def _(pe):
                pe.sem_inc(made, 2)
                if loads:
                    pe.wait_ge(loaded, 16 * len(loads))

                def one(t, u):
                    pe.wait_ge(taken, t + 1)
                    pe.wait_ge(staged, t * ns + ns)
                    for j, (src, w, bias, n) in enumerate(groups):
                        k = [x is src for x in srcs].index(True)
                        for f in range(src.shape[1]):
                            ins = nc.tensor.matmul(ps[j][:, u, 0:n], lhs[k][:, u, f, :], w[:, f, 0:n],
                                                   start=f == 0, stop=bias is None and f == src.shape[1] - 1)
                        if bias is not None:
                            ins = nc.tensor.matmul(ps[j][:, u, 0:n], kit.ones[0:1, :], bias, start=False, stop=True)
                    ins.then_inc(made, 1)

                with pe.Fori(0, PAIRS) as i:
                    for u in range(2):
                        one(i * 2 + u, u)
                one(NT - 1, 0)

            @block.vector
            def _(dve):
                link = Chain(dve, chain)
                dve.sem_inc(taken, 2)
                if loads:
                    dve.wait_ge(loaded, 16 * len(loads))
                if extra is not None and "ones" in extra:
                    for o in extra["ones"]:
                        link(nc.vector.memset(o, 1.0))

                def one(t, u, i):
                    dve.wait_ge(made, t + 3)
                    if sink:
                        dve.wait_ge(stored[u], i * dmas + dmas)
                    finish(dve, link, t, u, [p[:, u, :] for p in ps], extra).then_inc(taken, 1)
                    dve.wait_ge(taken, t + 3)

                with link.loop(PAIRS, 2 * links) as i:
                    for u in range(2):
                        one(i * 2 + u, u, i)
                one(NT - 1, 0, PAIRS)


def context(kit, name, ksrc, wk, vsrc, wv, halves, out, elu, den=None, col_scale=None, scale=1.0):
    nc = kit.nc
    KN = halves * P
    same = ksrc is vsrc
    srcs = [ksrc] if same else [ksrc, vsrc]
    with Stage(kit, name) as s:
        lhs = [s.sb(f"lhs{j}", [P, 2, x.shape[1], P]) for j, x in enumerate(srcs)]
        power = s.sb("power", [P, 2, KN])
        krow = s.sb("krow", [P, 2, KN])
        vrow = s.sb("vrow", [P, 2, halves, P + 1])
        zero = s.sb("zero", [P, P + 1])
        inv = s.sb("inv", [P, halves])
        ps_k = s.ps("ps_k", [P, 2, 512])
        ps_v = s.ps("ps_v", [P, 2, 512])
        ps_c = s.ps("ps_c", [P, halves, 512])
        staged, made, lowered, raised, taken, summed, set_up, chain, ready = (
            s.sem(n) for n in ("staged", "made", "lowered", "raised", "taken", "summed", "set_up", "chain", "ready"))
        ns = len(srcs)
        with nc.Block() as block:

            @block.gpsimd
            def _(pool):
                pool.sem_inc(set_up, 1)
                with pool.Fori(0, PAIRS) as i:
                    for u in range(2):
                        pool.wait_ge(made, i * 2 + (u + 1))
                        pool.wait_ge(set_up, 1)
                        for j, x in enumerate(srcs):
                            nc.gpsimd.tensor_copy(lhs[j][:, u], x[:, :, ds(i * 2 * P + u * P, P)]).then_inc(staged, 1)
                pool.wait_ge(made, 2 * PAIRS + 1)
                for j, x in enumerate(srcs):
                    nc.gpsimd.tensor_copy(lhs[j][:, 0], x[:, :, (NT - 1) * P:NP]).then_inc(staged, 1)

            @block.tensor
            def _(pe):
                pe.sem_inc(made, 2)
                pe.wait_ge(ready, 1)
                for h in range(halves):
                    nc.tensor.matmul(ps_c[:, h, 0:P + 1], kit.ident[:], zero[:], start=True, stop=True)

                def rows(t, u):
                    pe.wait_ge(taken, t + 1)
                    pe.wait_ge(staged, t * ns + ns)
                    for f in range(ksrc.shape[1]):
                        nc.tensor.matmul(ps_k[:, u, 0:KN], lhs[0][:, u, f, :], wk[:, f, :], start=f == 0,
                                         stop=f == ksrc.shape[1] - 1)
                    for f in range(vsrc.shape[1]):
                        ins = nc.tensor.matmul(ps_v[:, u, 0:KN], lhs[-1][:, u, f, :], wv[:, f, :], start=f == 0,
                                               stop=f == vsrc.shape[1] - 1)
                    ins.then_inc(made, 1)

                def outer(t, u, n=P):
                    pe.wait_ge(taken, t + 3)
                    for h in range(halves):
                        ins = nc.tensor.matmul(ps_c[:, h, 0:P + 1], krow[0:n, u, h * P:(h + 1) * P], vrow[0:n, u, h, :],
                                               start=False, stop=True, skip_group_check=True)
                    ins.then_inc(summed, 1)

                rows(0, 0)
                with pe.Fori(0, PAIRS) as i:
                    for u in range(2):
                        rows(i * 2 + (u + 1), (u + 1) % 2)
                        outer(i * 2 + u, u)
                outer(NT - 1, 0, LAST)

            @block.scalar
            def _(act):
                if not elu:
                    return

                def one(t, u):
                    act.wait_ge(made, t + 3)
                    act.wait_ge(taken, t + 1)
                    nc.scalar.activation(power[:, u, :], ps_k[:, u, 0:KN], ACT.Relu, scale=-1.0).then_inc(lowered, 1)
                    act.wait_ge(lowered, t + 1)
                    nc.scalar.activation(power[:, u, :], power[:, u, :], ACT.Exp, scale=-1.0).then_inc(raised, 1)

                with act.Fori(0, PAIRS) as i:
                    for u in range(2):
                        one(i * 2 + u, u)
                one(NT - 1, 0)

            @block.vector
            def _(dve):
                link = Chain(dve, chain)
                link(nc.vector.memset(zero[:], 0.0))
                link(nc.vector.memset(out[:], 0.0))
                if den is not None:
                    link(nc.vector.memset(den[:], 0.0))
                nc.vector.memset(vrow[:], 1.0).then_inc(ready, 1)
                dve.wait_ge(ready, 1)
                dve.sem_inc(taken, 2)
                dve.sem_inc(summed, 2)

                def one(t, u):
                    if elu:
                        dve.wait_ge(raised, t + 1)
                        dve.wait_ge(summed, t + 1)
                        nc.vector.scalar_tensor_tensor(out=krow[:, u, :], in0=ps_k[:, u, 0:KN], scalar=0.0,
                                                       in1=power[:, u, :], op0=ALU.max, op1=ALU.add)
                    else:
                        dve.wait_ge(made, t + 3)
                        dve.wait_ge(summed, t + 1)
                        nc.vector.tensor_copy(krow[:, u, :], ps_k[:, u, 0:KN])
                    nc.vector.tensor_copy(vrow[:, u, :, 0:P], ps_v[:, u, 0:KN].rearrange("p (h v) -> p h v", h=halves)
                                          ).then_inc(taken, 1)

                with link.loop(PAIRS, 0) as i:
                    for u in range(2):
                        one(i * 2 + u, u)
                one(NT - 1, 0)
                dve.wait_ge(summed, NT + 2)
                if col_scale is not None:
                    link(nc.vector.reciprocal(inv[:], col_scale))
                for h in range(halves):
                    to = out[:, h, h * P:(h + 1) * P]
                    link(nc.vector.scalar_tensor_tensor(
                        out=to, in0=ps_c[:, h, 0:P], scalar=inv[:, h:h + 1] if col_scale is not None else scale,
                        in1=kit.heads[:], op0=ALU.mult, op1=ALU.mult))
                    if col_scale is not None and scale != 1.0:
                        link(nc.vector.tensor_scalar(to, to, scale, None, ALU.mult))
                    if den is not None:
                        link(nc.vector.tensor_scalar(den[:, h, h * P:(h + 1) * P], kit.heads[:],
                                                     ps_c[:, h, P:P + 1], None, ALU.mult))


def soft_keys(kit, name, kt, total):
    nc = kit.nc
    halves = kt.shape[1]
    with Stage(kit, name) as s:
        top = s.sb("top", [P, halves])
        neg = s.sb("neg", [P, halves])
        maxed, raised, chain = s.sem("maxed"), s.sem("raised"), s.sem("chain")
        with nc.Block() as block:

            @block.vector
            def _(dve):
                link = Chain(dve, chain)
                link(nc.vector.tensor_reduce(top[:], kt[:, :, 0:N], X, ALU.max))
                nc.vector.tensor_scalar(neg[:], top[:], -1.0, None, ALU.mult).then_inc(maxed, 1)

            @block.scalar
            def _(act):
                act.wait_ge(maxed, 1)
                for h in range(halves):
                    nc.scalar.activation(kt[:, h, 0:N], kt[:, h, 0:N], ACT.Exp, bias=neg[:, h:h + 1],
                                         accum_out=total[:, h:h + 1]).then_inc(raised, 1)


def top_two(kit, name, logits, experts, comb, probs_weight):
    nc = kit.nc
    E_ = experts
    with Stage(kit, name) as s:
        p = s.sb("p", [P, NT, E_])
        code = s.sb("code", [P, NT, E_])
        eq = s.sb("eq", [P, NT, E_])
        one = [s.sb(f"one{j}", [P, NT, E_]) for j in range(2)]
        m = [s.sb(f"m{j}", [P, NT]) for j in range(2)]
        t = s.sb("t", [P, NT])
        w = [s.sb(f"w{j}", [P, NT]) for j in range(2)]
        ready, raised, chain = s.sem("ready"), s.sem("raised"), s.sem("chain")
        with nc.Block() as block:

            @block.scalar
            def _(act):
                act.wait_ge(ready, 1)
                nc.scalar.activation(p[:], p[:], ACT.Exp).then_inc(raised, 1)
                if not probs_weight:
                    act.wait_ge(ready, 2)
                    nc.scalar.activation(t[:], t[:], ACT.Exp).then_inc(raised, 1)

            @block.vector
            def _(dve):
                link = Chain(dve, chain)
                v = nc.vector
                link(v.memset(comb[:], 0.0))
                link(v.tensor_reduce(t[:], logits, X, ALU.max))
                v.tensor_tensor(p[:], logits, bcast(t[:], E_, 2), ALU.subtract).then_inc(ready, 1)
                link(v.tensor_scalar(code[:], bcast(kit.iota[:, 0:E_], NT, 1), -99.0, None, ALU.add))
                dve.wait_ge(raised, 1)
                link(v.tensor_reduce(t[:], p[:], X, ALU.add))
                link(v.reciprocal(t[:], t[:]))
                link(v.tensor_tensor(p[:], p[:], bcast(t[:], E_, 2), ALU.mult))
                for j in range(2):
                    link(v.tensor_reduce(m[j][:], p[:], X, ALU.max))
                    link(v.tensor_tensor(eq[:], p[:], bcast(m[j][:], E_, 2), ALU.is_equal))
                    link(v.tensor_tensor(eq[:], eq[:], code[:], ALU.mult))
                    link(v.tensor_reduce(t[:], eq[:], X, ALU.min))
                    link(v.tensor_tensor(one[j][:], code[:], bcast(t[:], E_, 2), ALU.is_equal))
                    if j == 0:
                        link(v.scalar_tensor_tensor(out=p[:], in0=one[0][:], scalar=-2.0, in1=p[:], op0=ALU.mult,
                                                    op1=ALU.add))
                if probs_weight:
                    link(v.tensor_tensor(t[:], m[0][:], m[1][:], ALU.add))
                    link(v.tensor_scalar(t[:], t[:], 1e-12, None, ALU.max))
                    link(v.reciprocal(t[:], t[:]))
                    for j in range(2):
                        link(v.tensor_tensor(w[j][:], m[j][:], t[:], ALU.mult))
                else:
                    v.tensor_tensor(t[:], m[1][:], m[0][:], ALU.subtract).then_inc(ready, 1)
                    dve.wait_ge(raised, 2)
                    link(v.tensor_scalar(w[0][:], t[:], 1.0, None, ALU.add))
                    link(v.reciprocal(w[0][:], w[0][:]))
                    link(v.tensor_tensor(w[1][:], w[0][:], t[:], ALU.mult))
                for j in range(2):
                    link(v.tensor_tensor(one[j][:], one[j][:], bcast(w[j][:], E_, 2), ALU.mult))
                link(v.tensor_tensor(comb[:, :, 0:E_], one[0][:], one[1][:], ALU.add))


def experts(kit, name, xnt, x, weights, biases, last_bias, comb_t, func):
    nc = kit.nc
    EX = weights[0].shape[1]
    HB = weights[0].shape[3] // P
    hid = len(weights) - 1
    B = 2 if EX > 1 else 1
    A = EX * hid * HB
    assert EX % B == 0 and A % 4 == 0
    with Stage(kit, name) as s:
        hidden = [s.sb(f"hidden{j}", [P, B, HB, CW]) for j in range(hid)]
        gated_h = s.sb("gated_h", [P, B, HB, CW])
        ps_h = s.ps("ps_h", [P, 4, 512])
        ps_g = s.ps("ps_g", [P, 512])
        ps_o = s.ps("ps_o", [P, 2, 512])
        made, taken, gate_made, gated, result, added = (
            s.sem(n) for n in ("made", "taken", "gate_made", "gated", "result", "added"))
        with nc.Block() as block:

            @block.tensor
            def _(pe):
                with pe.Fori(0, NC) as c:

                    def layer(e, l):
                        a = (e * hid + l) * HB
                        if l:
                            pe.wait_ge(taken, c * A + (a + 4))
                        src = [xnt[:, f, ds(c * CW, CW)] for f in range(2)] if l == 0 else \
                            [hidden[l - 1][:, e % B, f, :] for f in range(HB)]
                        for o in range(HB):
                            pe.wait_ge(taken, c * A + (a + o + 1))
                            for f, r in enumerate(src):
                                ins = nc.tensor.matmul(ps_h[:, (a + o) % 4, 0:CW], weights[l][:, e, f, o * P:(o + 1) * P],
                                                       r, start=f == 0, stop=f == len(src) - 1)
                            ins.then_inc(made, 1)

                    def gate(e):
                        pe.wait_ge(gated, c * EX + (e + B))
                        nc.tensor.matmul(ps_g[:, 0:CW], kit.pick[:, e, :], comb_t[:, ds(c * CW, CW)], start=True,
                                         stop=True).then_inc(gate_made, 1)

                    def out(e):
                        pe.wait_ge(gated, c * EX + (e + B + 1))
                        if e == 0:
                            pe.wait_ge(added, c + 1)
                        for o in range(2):
                            for f in range(HB):
                                nc.tensor.matmul(ps_o[:, o, 0:CW], weights[hid][:, e, f, o * P:(o + 1) * P],
                                                 gated_h[:, e % B, f, :], start=e == 0 and f == 0, stop=False)
                            if e == EX - 1:
                                ins = nc.tensor.matmul(ps_o[:, o, 0:CW], last_bias[:, o * P:(o + 1) * P],
                                                       comb_t[:, ds(c * CW, CW)], start=False, stop=True)
                                if o == 1:
                                    ins.then_inc(result, 1)

                    for l in range(hid):
                        layer(0, l)
                    for e in range(EX):
                        if e + 1 < EX:
                            layer(e + 1, 0)
                        gate(e)
                        out(e)
                        if e + 1 < EX:
                            for l in range(1, hid):
                                layer(e + 1, l)

            @block.scalar
            def _(act):
                act.sem_inc(taken, 4)
                with act.Fori(0, NC) as c:
                    for e in range(EX):
                        for l in range(hid):
                            for o in range(HB):
                                a = (e * hid + l) * HB + o
                                act.wait_ge(made, c * A + (a + 1))
                                if l == hid - 1 and o == 0:
                                    act.wait_ge(gated, c * EX + (e + 1))
                                nc.scalar.activation(hidden[l][:, e % B, o, :], ps_h[:, a % 4, 0:CW], func,
                                                     bias=biases[l][:, e, o:o + 1]).then_inc(taken, 1)

            @block.vector
            def _(dve):
                dve.sem_inc(gated, B)
                dve.sem_inc(added, 1)
                with dve.Fori(0, NC) as c:
                    for e in range(EX):
                        dve.wait_ge(gate_made, c * EX + (e + 1))
                        dve.wait_ge(taken, c * A + ((e + 1) * hid * HB + 4))
                        nc.vector.tensor_tensor(gated_h[:, e % B], hidden[hid - 1][:, e % B],
                                                bcast(ps_g[:, 0:CW], HB, 1), ALU.mult).then_inc(gated, 1)
                    dve.wait_ge(result, c + 1)
                    to = x[:, :, ds(c * CW, CW)]
                    nc.vector.tensor_tensor(to, ps_o[:, :, 0:CW], to, ALU.add).then_inc(added, 1)
                    dve.wait_ge(added, c + 2)


def composite_scores(kit, name, w_pair, w_rows, attn_t):
    nc = kit.nc
    with Stage(kit, name) as s:
        rows = s.sb("rows", [64, 2, D])
        a = s.sb("a", [64, 4])
        ps = s.ps("ps", [P, 4, 4])
        loaded, made, placed = s.sem("loaded"), s.sem("made"), s.sem("placed")
        with nc.Block() as block:

            @block.sync
            def _(sp):
                sp.dma_start(rows[:], w_rows).then_inc(loaded, 16)
                sp.dma_start(a[:], attn_t).then_inc(loaded, 16)
                sp.dma_start(w_pair[:, :, 0:64], kit.dram["L0_w_fwd"]).then_inc(loaded, 16)
                sp.dma_start(w_pair[:, :, 68:132], kit.dram["L0_w_rev"]).then_inc(loaded, 16)
                sp.wait_ge(loaded, 64)

            @block.tensor
            def _(pe):
                pe.wait_ge(loaded, 64)
                for d in range(2):
                    for f in range(2):
                        ins = nc.tensor.matmul(ps[:, 2 * d + f, :], rows[:, d, f * P:(f + 1) * P], a[:], start=True,
                                               stop=True)
                ins.then_inc(made, 1)

            @block.vector
            def _(dve):
                dve.wait_ge(made, 1)
                for d in range(2):
                    nc.vector.tensor_copy(w_pair[:, :, 68 * d + 64:68 * d + 68], ps[:, 2 * d:2 * d + 2, :])


def finish_directed(kit, name, acc, mx, out):
    nc = kit.nc
    H, V = 4, 65
    with Stage(kit, name) as s:
        top = s.sb("top", [P, H])
        top_t = s.sb("top_t", [H, 1])
        wide = s.sb("wide", [H, P])
        diag = s.sb("diag", [H, H])
        f = s.sb("f", [P, NT, H])
        z = s.sb("z", [P, NT, H])
        ps_t = s.ps("ps_t", [P, 512])
        ps_b = s.ps("ps_b", [P, 512])
        maxed, turned, spread, fallen, raised, chain, all_max = (
            s.sem(n) for n in ("maxed", "turned", "spread", "fallen", "raised", "chain", "all_max"))
        with nc.Block() as block:

            @block.vector
            def _(dve):
                link = Chain(dve, chain)
                v = nc.vector
                v.tensor_reduce(top[:], mx.rearrange("p t h -> p h t"), X, ALU.max).then_inc(maxed, 1)
                dve.wait_ge(turned, 1)
                link(v.tensor_reduce(top_t[:], ps_t[0:H, 0:P], X, ALU.max))
                v.tensor_scalar(diag[:], kit.ident[0:H, 0:H], top_t[:, 0:1], None, ALU.mult).then_inc(all_max, 1)
                dve.wait_ge(spread, 1)
                v.tensor_tensor(f[:], mx, bcast(ps_b[:, 0:H], NT, 1), ALU.subtract).then_inc(fallen, 1)
                dve.wait_ge(raised, 1)
                a4 = acc.rearrange("p t (h v) -> p t h v", h=H)
                link(v.tensor_tensor(z[:], a4[:, :, :, V - 1], f[:], ALU.mult))
                link(v.tensor_scalar(z[:], z[:], 1e-10, None, ALU.add))
                link(v.reciprocal(z[:], z[:]))
                link(v.tensor_tensor(z[:], z[:], f[:], ALU.mult))
                for h in range(H):
                    v.tensor_tensor(out[:, :, h * 64:(h + 1) * 64], a4[:, :, h, 0:64], bcast(z[:, :, h], 64, 2),
                                    ALU.mult)

            @block.tensor
            def _(pe):
                pe.wait_ge(maxed, 1)
                nc.tensor.transpose(ps_t[0:H, 0:P], top[:], kit.ident[:]).then_inc(turned, 1)
                pe.wait_ge(all_max, 1)
                nc.tensor.matmul(ps_b[:, 0:H], kit.ones[0:H, :], diag[:], start=True, stop=True).then_inc(spread, 1)

            @block.scalar
            def _(act):
                act.wait_ge(fallen, 1)
                nc.scalar.activation(f[:], f[:], ACT.Exp).then_inc(raised, 1)


def finish_softmax(kit, name, acc, heads, width, out, own=None, mx=None, own_score=None, own_dram=None):
    nc = kit.nc
    H, V = heads, width
    with Stage(kit, name) as s:
        z = s.sb("z", [P, NT, H])
        if own_dram is not None:
            own = s.sb("own", [P, NT, H * V])
            new = s.sb("new", [P, NT, H])
            fall = s.sb("fall", [P, 2, NT, H])
        loaded, fallen, raised, chain = (s.sem(n) for n in ("loaded", "fallen", "raised", "chain"))
        with nc.Block() as block:

            @block.sync
            def _(sp):
                if own_dram is not None:
                    sp.dma_start(own[:], own_dram[0:NP, 0:H * V].rearrange("(t p) w -> p t w", p=P)
                                 ).then_inc(loaded, 16)
                    sp.wait_ge(loaded, 16)

            @block.scalar
            def _(act):
                if own_dram is not None:
                    act.wait_ge(fallen, 1)
                    nc.scalar.activation(fall[:], fall[:], ACT.Exp).then_inc(raised, 1)

            @block.vector
            def _(dve):
                link = Chain(dve, chain)
                v = nc.vector
                a4 = acc.rearrange("p t (h v) -> p t h v", h=H)
                if own_dram is not None:
                    link(v.tensor_tensor(new[:], mx, own_score, ALU.max))
                    v.tensor_tensor(fall[:, 0], mx, new[:], ALU.subtract)
                    v.tensor_tensor(fall[:, 1], own_score, new[:], ALU.subtract).then_inc(fallen, 1)
                    dve.wait_ge(loaded, 16)
                    dve.wait_ge(raised, 1)
                    o4 = own[:].rearrange("p t (h v) -> p t h v", h=H)
                    for h in range(H):
                        v.tensor_tensor(a4[:, :, h], a4[:, :, h], bcast(fall[:, 0, :, h], V, 2), ALU.mult)
                        link(v.tensor_tensor(o4[:, :, h], o4[:, :, h], bcast(fall[:, 1, :, h], V, 2), ALU.mult))
                    link(v.tensor_tensor(acc, acc, own[:], ALU.add))
                link(v.tensor_scalar(z[:], a4[:, :, :, V - 1], 1e-30, None, ALU.max))
                link(v.reciprocal(z[:], z[:]))
                for h in range(H):
                    v.tensor_tensor(out[:, :, h * (V - 1):(h + 1) * (V - 1)], a4[:, :, h, 0:V - 1],
                                    bcast(z[:, :, h], V - 1, 2), ALU.mult)


def choose_half(kit, name, weight_all, comb, keep):
    nc = kit.nc
    with Stage(kit, name) as s:
        mine = s.sb("mine", [P, NT])
        before = s.sb("before", [P, NP])
        junk = s.sb("junk", [P, N])
        junk2 = s.sb("junk2", [P, N])
        above = s.sb("above", [P, NT])
        tied = s.sb("tied", [P, NT])
        chain = s.sem("chain")
        with nc.Block() as block:

            @block.vector
            def _(dve):
                link = Chain(dve, chain)
                v = nc.vector
                link(v.memset(comb[:], 0.0))
                link(v.memset(before[:], 0.0))
                with link.loop(NT, 5) as t:
                    one = ds(t, 1)
                    link(v.scalar_tensor_tensor(out=junk[:, 0:P], in0=weight_all[:, ds(t * P, P)], scalar=1.0,
                                                in1=kit.ident[:], op0=ALU.mult, op1=ALU.mult, accum_out=mine[:, one]))
                    link(v.tensor_scalar(before[:, ds(t * P, P)], kit.earlier[:], 0.0, None, ALU.add))
                    link(v.scalar_tensor_tensor(out=junk[:], in0=weight_all[:, 0:N], scalar=mine[:, one], in1=before[:, 0:N],
                                                op0=ALU.is_equal, op1=ALU.mult, accum_out=tied[:, one]))
                    link(v.tensor_scalar(junk2[:], weight_all[:, 0:N], mine[:, one], 0.0, ALU.is_gt, ALU.add,
                                         accum_out=above[:, one]))
                    link(v.tensor_scalar(before[:, ds(t * P, P)], kit.earlier[:], 0.0, 1.0, ALU.mult, ALU.add))
                link(v.tensor_tensor(above[:], above[:], tied[:], ALU.add))
                v.scalar_tensor_tensor(out=comb[:, :, 0], in0=above[:], scalar=float(keep), in1=mine[:],
                                       op0=ALU.is_lt, op1=ALU.mult)


def gates(kit, name, agg, w, bias, hn):
    nc = kit.nc
    with Stage(kit, name) as s:
        gate = s.sb("gate", [P, 6, CW])
        cell = s.sb("cell", [P, 2, CW])
        th = s.sb("th", [P, 2, CW])
        ps = s.ps("ps", [P, 6, 512])
        b = s.sb("b", [P, 6])
        made, taken, celled, bent, out_done = (
            s.sem(n) for n in ("made", "taken", "celled", "bent", "out_done"))
        with nc.Block() as block:

            @block.tensor
            def _(pe):
                with pe.Fori(0, NC) as c:
                    for o in range(6):
                        pe.wait_ge(taken, c * 6 + (o + 1))
                        for f in range(2):
                            ins = nc.tensor.matmul(ps[:, o, 0:CW], w[:, f, o * P:(o + 1) * P],
                                                   agg[:, f, ds(c * CW, CW)], start=f == 0, stop=f == 1)
                        ins.then_inc(made, 1)

            @block.scalar
            def _(act):
                act.sem_inc(taken, 6)
                act.wait_ge(celled, 1)
                with act.Fori(0, NC) as c:
                    for o in range(6):
                        act.wait_ge(made, c * 6 + (o + 1))
                        if o == 0:
                            act.wait_ge(out_done, c + 1)
                        nc.scalar.activation(gate[:, o, :], ps[:, o, 0:CW], ACT.Tanh if o in (2, 3) else ACT.Sigmoid,
                                             bias=b[:, o:o + 1]).then_inc(taken, 1)
                    act.wait_ge(celled, c + 2)
                    nc.scalar.activation(th[:], cell[:], ACT.Tanh).then_inc(bent, 1)

            @block.vector
            def _(dve):
                nc.vector.tensor_tensor(b[:], bias[:, 0, :], bias[:, 1, :], ALU.add).then_inc(celled, 1)
                dve.sem_inc(out_done, 1)
                with dve.Fori(0, NC) as c:
                    dve.wait_ge(taken, c * 6 + 12)
                    nc.vector.tensor_tensor(cell[:], gate[:, 0:2], gate[:, 2:4], ALU.mult).then_inc(celled, 1)
                    dve.wait_ge(bent, c + 1)
                    nc.vector.tensor_tensor(hn[:, :, ds(c * CW, CW)], gate[:, 4:6], th[:], ALU.mult).then_inc(out_done, 1)
                    dve.wait_ge(out_done, c + 2)


def softmax_queries(kit, name, q, out):
    nc = kit.nc
    with Stage(kit, name) as s:
        m = s.sb("m", [P, 2, 8])
        shifted = s.sb("shifted", [P, 2, D])
        e = s.sb("e", [P, 2, D])
        lowered, raised, divided, chain = (s.sem(n) for n in ("lowered", "raised", "divided", "chain"))
        with nc.Block() as block:

            @block.vector
            def _(dve):
                link = Chain(dve, chain)
                v = nc.vector

                def by_head(a):
                    return a.rearrange("p (h v) -> p h v", v=32)

                def lower(t, u):
                    qt = by_head(q[:, ds(t, 1), :].squeeze(1))
                    link(v.tensor_reduce(m[:, u, :], qt, X, ALU.max))
                    v.tensor_tensor(by_head(shifted[:, u, :]), qt, bcast(m[:, u, :], 32, 2),
                                    ALU.subtract).then_inc(lowered, 1)

                def divide(t, u):
                    dve.wait_ge(raised, t + 1)
                    link(v.tensor_reduce(m[:, u, :], by_head(e[:, u, :]), X, ALU.add))
                    link(v.reciprocal(m[:, u, :], m[:, u, :]))
                    v.tensor_tensor(by_head(out[:, ds(t, 1), :].squeeze(1)), by_head(e[:, u, :]), bcast(m[:, u, :], 32, 2),
                                    ALU.mult).then_inc(divided, 1)
                    dve.wait_ge(divided, t + 1)

                with link.loop(PAIRS, 6) as i:
                    lower(i * 2, 0)
                    lower(i * 2 + 1, 1)
                    divide(i * 2, 0)
                    divide(i * 2 + 1, 1)
                lower(NT - 1, 0)
                divide(NT - 1, 0)

            @block.scalar
            def _(act):
                def one(t, u):
                    act.wait_ge(lowered, t + 1)
                    nc.scalar.activation(e[:, u, :], shifted[:, u, :], ACT.Exp).then_inc(raised, 1)

                with act.Fori(0, PAIRS) as i:
                    one(i * 2, 0)
                    one(i * 2 + 1, 1)
                one(NT - 1, 0)


CAP = -(-N * 5 // (4 * 8))
CAPT = -(-CAP // P)
EXPERTS = 8


def assign(kit, name, logits, place, back, scale):
    nc = kit.nc
    E_ = EXPERTS
    with Stage(kit, name) as s:
        p = s.sb("p", [P, NT, E_])
        code = s.sb("code", [P, NT, E_])
        one = s.sb("one", [P, NT, E_])
        pos = s.sb("pos", [P, NT, E_])
        run = s.sb("run", [P, NT, E_])
        zeros = s.sb("zeros", [P, NT])
        t = s.sb("t", [P, NT])
        best = s.sb("best", [P, NT])
        kept = s.sb("kept", [P, NT])
        spare = s.sb("spare", [P, NT])
        real = s.sb("real", [P, NT])
        row = s.sb("row", [P, NT])
        row_i = s.sb("row_i", [P, NT], I32)
        ps_in = s.ps("ps_in", [P, 512])
        ps_all = s.ps("ps_all", [P, 512])
        loaded, ready, raised, chosen, counted, chain = (
            s.sem(n) for n in ("loaded", "ready", "raised", "chosen", "counted", "chain"))
        with nc.Block() as block:

            @block.sync
            def _(sp):
                sp.dma_start(spare[:], kit.dram["node_spare"]).then_inc(loaded, 16)
                sp.dma_start(real[:], kit.dram["node_real"]).then_inc(loaded, 16)
                sp.wait_ge(loaded, 32)

            @block.scalar
            def _(act):
                act.wait_ge(ready, 1)
                nc.scalar.activation(p[:], p[:], ACT.Exp).then_inc(raised, 1)

            @block.tensor
            def _(pe):
                pe.wait_ge(chosen, 1)
                flat = one[:].rearrange("p t e -> p (t e)")
                nc.tensor.matmul(ps_in[:, 0:NT * E_], kit.later[:], flat, start=True, stop=True)
                nc.tensor.matmul(ps_all[:, 0:NT * E_], kit.ones[:], flat, start=True, stop=True).then_inc(counted, 1)

            @block.vector
            def _(dve):
                link = Chain(dve, chain)
                v = nc.vector
                dve.wait_ge(loaded, 32)
                link(v.memset(zeros[:], 0.0))
                link(v.tensor_reduce(t[:], logits, X, ALU.max))
                v.tensor_tensor(p[:], logits, bcast(t[:], E_, 2), ALU.subtract).then_inc(ready, 1)
                link(v.tensor_scalar(code[:], bcast(kit.iota[:, 0:E_], NT, 1), -99.0, None, ALU.add))
                dve.wait_ge(raised, 1)
                link(v.tensor_reduce(t[:], p[:], X, ALU.add))
                link(v.reciprocal(t[:], t[:]))
                link(v.tensor_tensor(p[:], p[:], bcast(t[:], E_, 2), ALU.mult))
                link(v.tensor_reduce(best[:], p[:], X, ALU.max))
                link(v.tensor_tensor(one[:], p[:], bcast(best[:], E_, 2), ALU.is_equal))
                link(v.tensor_tensor(one[:], one[:], code[:], ALU.mult))
                link(v.tensor_reduce(t[:], one[:], X, ALU.min))
                link(v.tensor_tensor(one[:], code[:], bcast(t[:], E_, 2), ALU.is_equal))
                v.tensor_tensor(one[:], one[:], bcast(real[:], E_, 2), ALU.mult).then_inc(chosen, 1)
                dve.wait_ge(counted, 1)
                all_t = ps_all[:, 0:NT * E_].rearrange("p (t e) -> p t e", e=E_)
                link(v.tensor_copy(pos[:], all_t))
                for e in range(E_):
                    link(v.tensor_tensor_scan(run[:, :, e], zeros[:], pos[:, :, e], 0.0, ALU.add, ALU.add))
                link(v.tensor_tensor(run[:], run[:], pos[:], ALU.subtract))
                link(v.tensor_tensor(pos[:], ps_in[:, 0:NT * E_].rearrange("p (t e) -> p t e", e=E_), run[:], ALU.add))
                link(v.tensor_tensor(pos[:], pos[:], one[:], ALU.mult))
                link(v.tensor_reduce(row[:], pos[:], X, ALU.add))
                link(v.tensor_scalar(kept[:], row[:], float(CAP), None, ALU.is_lt))
                link(v.tensor_tensor(kept[:], kept[:], real[:], ALU.mult))
                link(v.tensor_scalar(t[:], t[:], 99.0, float(CAPT * P), ALU.add, ALU.mult))
                link(v.tensor_tensor(row[:], row[:], t[:], ALU.add))
                v.tensor_tensor(back[:], row[:], kept[:], ALU.mult)
                link(v.tensor_tensor(row[:], row[:], spare[:], ALU.subtract))
                link(v.tensor_tensor(row[:], row[:], kept[:], ALU.mult))
                link(v.tensor_tensor(row[:], row[:], spare[:], ALU.add))
                link(v.tensor_copy(place[:], row[:]))
                v.tensor_tensor(scale[:], best[:], kept[:], ALU.mult)


def move_rows(kit, name, rows, table, place, scatter, blank=None):
    nc = kit.nc
    with Stage(kit, name) as s:
        zero = s.sb("zero", [P, 2048])
        gate = s.sb("gate", [P, 2])
        cleared, moved, cleaned = s.sem("cleared"), s.sem("moved"), s.sem("cleaned")
        with nc.Block() as block:

            @block.vector
            def _(dve):
                nc.vector.memset(zero[:], 0.0).then_inc(cleared, 1)

            @block.sync
            def _(sp):
                sp.wait_ge(cleared, 1)
                if scatter:
                    n = table.shape[0] * D // (P * 2048)
                    for j in range(n):
                        sp.dma_start(table[j * 1024:(j + 1) * 1024, :].rearrange("(p a) d -> p (a d)", p=P),
                                     zero[:]).then_inc(cleaned, 16)
                    sp.wait_ge(cleaned, 16 * n)

            @block.gpsimd
            def _(pool):
                if scatter:
                    pool.wait_ge(cleaned, 16 * (table.shape[0] * D // (P * 2048)))
                for t in range(NT):
                    at_ = bass.IndirectOffsetOnAxis(place[:, t:t + 1], 0)
                    if scatter:
                        pool.indirect_dma_start(table, at_, rows[:, t, :], None).then_inc(moved, 16)
                    else:
                        pool.indirect_dma_start(rows[:, t, :], None, table, at_).then_inc(moved, 16)
                pool.wait_ge(moved, 16 * NT)


def run_experts(kit, name, given, result):
    nc, dram = kit.nc, kit.dram
    HB = 8
    R = CAPT * P
    with Stage(kit, name) as s:
        w1 = s.sb("w1", [P, 2, 2, HB * P])
        w2 = s.sb("w2", [P, 2, HB, D])
        b1 = s.sb("b1", [P, 2, HB])
        b2 = s.sb("b2", [1, 2, D])
        got = s.sb("got", [P, 2, CAPT, D])
        got_t = s.sb("got_t", [P, 2, R])
        hidden = s.sb("hidden", [P, HB, R])
        rows = s.sb("rows", [P, 2, CAPT, D])
        ps_t = s.ps("ps_t", [P, 2, 512])
        ps_h = s.ps("ps_h", [P, 4, 512])
        ps_o = s.ps("ps_o", [P, 2, 512])
        loaded = [s.sem(f"loaded{b}") for b in range(2)]
        stored = [s.sem(f"stored{b}") for b in range(2)]
        turned, copied, made, taken, summed, written = (
            s.sem(n) for n in ("turned", "copied", "made", "taken", "summed", "written"))
        with nc.Block() as block:

            @block.sync
            def _(sp):
                def load(e, b):
                    for to, frm in ((w1[:, b], dram["L3_w1"][ds(e, 1)].squeeze(0)),
                                    (w2[:, b], dram["L3_w2"][ds(e, 1)].squeeze(0)),
                                    (b1[:, b], dram["L3_b1"][ds(e, 1)].squeeze(0)),
                                    (b2[:, b], dram["L3_b2"][ds(e, 1)]),
                                    (got[:, b], given[ds(e * R, R), :].rearrange("(a p) d -> p a d", p=P))):
                        sp.dma_start(to, frm).then_inc(loaded[b], 16)

                def store(e, b):
                    sp.wait_ge(written, e * CAPT + (CAPT + 2))
                    sp.dma_start(result[ds(e * R, R), :].rearrange("(a p) d -> p a d", p=P),
                                 rows[:, b]).then_inc(stored[b], 16)

                load(0, 0)
                load(1, 1)
                with sp.Fori(0, EXPERTS // 2 - 1) as i:
                    for b in range(2):
                        store(i * 2 + b, b)
                        load(i * 2 + (b + 2), b)
                for b in range(2):
                    store(EXPERTS - 2 + b, b)
                for b in range(2):
                    sp.wait_ge(stored[b], 16 * (EXPERTS // 2 + 1))

            @block.tensor
            def _(pe):
                with pe.Fori(0, EXPERTS // 2) as i:
                    for b in range(2):
                        e = i * 2 + b
                        pe.wait_ge(loaded[b], i * 80 + 80)
                        for a in range(CAPT):
                            pe.wait_ge(copied, e * CAPT + (a + 1))
                            for f in range(2):
                                ins = nc.tensor.transpose(ps_t[:, a % 2, f * P:(f + 1) * P],
                                                          got[:, b, a, f * P:(f + 1) * P], kit.ident[:])
                            ins.then_inc(turned, 1)
                        pe.wait_ge(copied, e * CAPT + (CAPT + 2))
                        for o in range(HB):
                            pe.wait_ge(taken, e * HB + (o + 1))
                            for f in range(2):
                                ins = nc.tensor.matmul(ps_h[:, o % 4, 0:R], w1[:, b, f, o * P:(o + 1) * P],
                                                       got_t[:, f, :], start=f == 0, stop=f == 1)
                            ins.then_inc(made, 1)
                        pe.wait_ge(taken, e * HB + (HB + 4))
                        for a in range(CAPT):
                            pe.wait_ge(written, e * CAPT + (a + 1))
                            for f in range(HB):
                                nc.tensor.matmul(ps_o[:, a % 2, 0:D], hidden[:, f, a * P:(a + 1) * P], w2[:, b, f, :],
                                                 start=f == 0, stop=False)
                            nc.tensor.matmul(ps_o[:, a % 2, 0:D], kit.ones[0:1, :], b2[:, b, :], start=False,
                                             stop=True).then_inc(summed, 1)

            @block.scalar
            def _(act):
                act.sem_inc(taken, 4)
                with act.Fori(0, EXPERTS // 2) as i:
                    for b in range(2):
                        e = i * 2 + b
                        act.wait_ge(loaded[b], i * 80 + 80)
                        for o in range(HB):
                            act.wait_ge(made, e * HB + (o + 1))
                            nc.scalar.activation(hidden[:, o, :], ps_h[:, o % 4, 0:R], ACT.Relu,
                                                 bias=b1[:, b, o:o + 1]).then_inc(taken, 1)

            @block.vector
            def _(dve):
                dve.sem_inc(copied, 2)
                dve.sem_inc(written, 2)
                for b in range(2):
                    dve.sem_inc(stored[b], 16)
                with dve.Fori(0, EXPERTS // 2) as i:
                    for b in range(2):
                        e = i * 2 + b
                        for a in range(CAPT):
                            dve.wait_ge(turned, e * CAPT + (a + 1))
                            nc.vector.tensor_copy(got_t[:, :, a * P:(a + 1) * P],
                                                  ps_t[:, a % 2, 0:D].rearrange("p (f n) -> p f n", f=2)
                                                  ).then_inc(copied, 1)
                        dve.wait_ge(stored[b], i * 16 + 16)
                        for a in range(CAPT):
                            dve.wait_ge(summed, e * CAPT + (a + 1))
                            nc.vector.tensor_copy(rows[:, b, a, :], ps_o[:, a % 2, 0:D]).then_inc(written, 1)


def scale_rows(kit, name, rows, scale):
    nc = kit.nc
    with Stage(kit, name) as s:
        with nc.Block() as block:

            @block.vector
            def _(dve):
                nc.vector.tensor_tensor(rows, rows, bcast(scale, rows.shape[2], 2), ALU.mult)


def constants(kit, ctx):
    nc = kit.nc
    kit.ident = ctx.enter_context(nc.sbuf_tensor("ident", [P, P], F32))
    kit.iota = ctx.enter_context(nc.sbuf_tensor("iota", [P, P], F32))
    kit.earlier = ctx.enter_context(nc.sbuf_tensor("earlier", [P, P], F32))
    kit.later = ctx.enter_context(nc.sbuf_tensor("later", [P, P], F32))
    kit.tile_no = ctx.enter_context(nc.sbuf_tensor("tile_no", [P, ST], F32))
    kit.ones = ctx.enter_context(nc.sbuf_tensor("ones", [P, P], F32))
    kit.mean = ctx.enter_context(nc.sbuf_tensor("mean", [P, P], F32))
    kit.eps = ctx.enter_context(nc.sbuf_tensor("eps", [P, 1], F32))
    kit.heads = ctx.enter_context(nc.sbuf_tensor("heads", [P, P], F32))
    kit.pick = ctx.enter_context(nc.sbuf_tensor("pick", [P, 8, P], F32))
    with Stage(kit, "constants") as s:
        loaded, filled = s.sem("loaded"), s.sem("filled")
        with nc.Block() as block:

            @block.sync
            def _(sp):
                for name, to in (("ident", kit.ident), ("iota", kit.iota), ("earlier", kit.earlier),
                                 ("later", kit.later), ("tile_no", kit.tile_no), ("heads", kit.heads), ("pick", kit.pick)):
                    sp.dma_start(to[:], kit.dram[name]).then_inc(loaded, 16)
                sp.wait_ge(loaded, 16 * 7)

            @block.vector
            def _(dve):
                nc.vector.memset(kit.ones[:], 1.0).then_inc(filled, 1)
                nc.vector.memset(kit.mean[:], 1.0 / D).then_inc(filled, 1)
                nc.vector.memset(kit.eps[:], 1e-5).then_inc(filled, 1)


def load(kit, name, pairs):
    nc = kit.nc
    with Stage(kit, name) as s:
        loaded = s.sem("loaded")
        with nc.Block() as block:

            @block.sync
            def _(sp):
                for to, frm in pairs:
                    sp.dma_start(to, frm).then_inc(loaded, 16)
                sp.wait_ge(loaded, 16 * len(pairs))


def clear(kit, name, buf):
    nc = kit.nc
    with Stage(kit, name) as s:
        with nc.Block() as block:

            @block.vector
            def _(dve):
                nc.vector.memset(buf, 0.0)


def add_in(kit, name, x, other, bias=None):
    nc = kit.nc
    with Stage(kit, name) as s:
        with nc.Block() as block:

            @block.vector
            def _(dve):
                for f in range(2):
                    nc.vector.scalar_tensor_tensor(out=x[:, f, :], in0=other[:, f, :],
                                                   scalar=bias[:, f:f + 1] if bias is not None else 0.0,
                                                   in1=x[:, f, :], op0=ALU.add, op1=ALU.add)


def stretch(kit, name, x, gamma, beta):
    nc = kit.nc
    with Stage(kit, name) as s:
        with nc.Block() as block:

            @block.vector
            def _(dve):
                for f in range(2):
                    nc.vector.tensor_scalar(x[:, f, :], x[:, f, :], gamma[:, f:f + 1], beta[:, f:f + 1], ALU.mult,
                                            ALU.add)


def elu_in_place(kit, name, x):
    nc = kit.nc
    with Stage(kit, name) as s:
        e = s.sb("e", [P, 2, NP])
        low, raised, chain = s.sem("low"), s.sem("raised"), s.sem("chain")
        with nc.Block() as block:

            @block.vector
            def _(dve):
                link = Chain(dve, chain)
                for f in range(2):
                    nc.vector.tensor_scalar(e[:, f, :], x[:, f, :], 0.0, None, ALU.min).then_inc(low, 1)
                for f in range(2):
                    dve.wait_ge(raised, f + 1)
                    link(nc.vector.tensor_scalar(e[:, f, :], e[:, f, :], -1.0, None, ALU.add))
                    nc.vector.scalar_tensor_tensor(out=x[:, f, :], in0=x[:, f, :], scalar=0.0, in1=e[:, f, :],
                                                   op0=ALU.max, op1=ALU.add)

            @block.scalar
            def _(act):
                for f in range(2):
                    act.wait_ge(low, f + 1)
                    nc.scalar.activation(e[:, f, :], e[:, f, :], ACT.Exp).then_inc(raised, 1)


class Memory:

    def __init__(self, kit):
        self.kit, self.ctx = kit, ExitStack()

    def __enter__(self):
        return self

    def __call__(self, name, shape, dt=F32):
        return self.ctx.enter_context(self.kit.nc.sbuf_tensor(name, shape, dt))[:]

    def loaded(self, *names):
        d = self.kit.dram
        self.kit.loads += 1
        bufs = [self(f"{n}_sb{self.kit.loads}", list(d[n].shape)) for n in names]
        load(self.kit, f"load{self.kit.loads}", list(zip(bufs, (d[n] for n in names))))
        return bufs

    def __exit__(self, *e):
        self.ctx.close()


def node_rows(table, t, first=0):
    return table[ds(t * P + first, P), :]


def layer0(kit, x, xn, slots, buckets, scratch):
    layernorm(kit, "L0_norm", x, xn)
    with Memory(kit) as m:
        w_pair = m("L0_w_pair", [P, 2, 136])
        composite_scores(kit, "L0_scores", w_pair, kit.dram["L0_w_rows"], kit.dram["L0_attn"])

        def finish(dve, link, t, u, banks, extra):
            return kit.nc.vector.tensor_copy(extra["row"][:, u, :], banks[0][:, 0:136])

        def sink(sp, t, u, extra, sem=None):
            if sp is not None:
                sp.dma_start(node_rows(scratch["L0"], t), extra["row"][:, u, :]).then_inc(sem, 16)
            return 1

        rows_of(kit, "L0_table", [(xn, w_pair, None, 136)], finish, sink=sink,
                setup=lambda s: {"row": s.sb("row", [P, 2, 136])})
    with Memory(kit) as m:
        acc, mx, rows = m("L0_acc", [P, NT, 260]), m("L0_mx", [P, NT, 4]), m("L0_rows", [P, NT, D])
        edge_pass(kit, "L0_edges", "dual", slots, buckets, scratch["L0"], R_OTHER, None, 4, 65, acc, mx)
        finish_directed(kit, "L0_finish", acc, mx, rows)
        turn_rows(kit, "L0_add", rows, x, add=True)
    with Memory(kit) as m:
        wq, wk, wv, wp, bp = m.loaded("L0_wq", "L0_wk", "L0_wv", "L0_wp", "L0_bp")
        linear_attention(kit, "L0_mix", m, xn, wq, wk, wv, floor=1e-6, plus=0.0, shrink=1.0,
                         out=lambda a: [Layer(wp, a, x, bias=bp, add=True)])
    layernorm(kit, "L0_norm2", x, xn)
    with Memory(kit) as m:
        comb_t = m("L0_comb_t", [P, NP])
        with Memory(kit) as m2:
            r1, rb1, r2, rb2 = m2.loaded("L0_r1", "L0_rb1", "L0_r2", "L0_rb2")
            rh = m2("L0_rh", [P, 1, NP])
            layers(kit, "L0_router", [Layer(r1, xn, rh, bias=rb1, func="relu")])
            route(kit, "L0", m2, rh, r2, rb2, 6, comb_t, False)
        e1, e2, e3, eb1, eb2, eb3 = m.loaded("L0_e1", "L0_e2", "L0_e3", "L0_eb1", "L0_eb2", "L0_eb3")
        experts(kit, "L0_experts", xn, x, [e1, e2, e3], [eb1, eb2], eb3, comb_t, ACT.Relu)


def route(kit, name, m, src, w, bias, n, comb_t, probs_weight):
    logits, comb = m(f"{name}_logits", [P, NT, n]), m(f"{name}_comb", [P, NT, 8])

    def finish(dve, link, t, u, banks, extra):
        return kit.nc.vector.tensor_scalar(logits[:, ds(t, 1), :].squeeze(1), banks[0][:, 0:n], 0.0, None, ALU.add)

    rows_of(kit, f"{name}_logit_rows", [(src, w, bias, n)], finish)
    top_two(kit, f"{name}_top", logits, n, comb, probs_weight)
    clear(kit, f"{name}_clear", comb_t)
    turn_rows(kit, f"{name}_comb_turn", comb, comb_t[0:8, :])


def linear_attention(kit, name, m, xn, wq, wk, wv, floor, plus, shrink, out):
    q = m(f"{name}_q", [P, 2, NP])
    ctx, den = m(f"{name}_ctx", [P, 2, D]), m(f"{name}_den", [P, 2, D])
    inv, a = m(f"{name}_inv", [P, 2, CW]), m(f"{name}_a", [P, 2, CW])
    layers(kit, f"{name}_queries", [Layer(wq, xn, q, func="elu1")])
    context(kit, f"{name}_context", xn, wk, xn, wv, 2, ctx, True, den=den, scale=1.0 / shrink)
    layers(kit, f"{name}_out", [Layer(den, q, inv, func="reciprocal", floor=floor, plus=plus),
                                Layer(ctx, q, a, func="times", other=inv, scale=shrink)] + out(a))


def layer1(kit, x, xn, slots, buckets, scratch):
    nc = kit.nc
    layernorm(kit, "L1_norm", x, xn)
    with Memory(kit) as m:
        wq, wkv, bq, bkv = m.loaded("L1_wq", "L1_wkv", "L1_bq", "L1_bkv")

        def setup(s):
            kv = s.sb("kv", [P, 2, 520])
            return {"kv": kv, "q": s.sb("q", [P, 2, D]), "ones": [kv[:]]}

        def finish(dve, link, t, u, banks, extra):
            kv = extra["kv"][:, u, :]
            nc.vector.tensor_copy(kv[:, 0:D], banks[0][:, 0:D])
            nc.vector.tensor_copy(kv[:, D:520].rearrange("p (h v) -> p h v", h=8)[:, :, 0:32],
                                  banks[0][:, D:2 * D].rearrange("p (h v) -> p h v", h=8))
            return nc.vector.tensor_scalar(extra["q"][:, u, :], banks[1][:, 0:D], 32.0 ** -0.5, None, ALU.mult)

        def sink(sp, t, u, extra, sem=None):
            if sp is not None:
                sp.dma_start(node_rows(scratch["L1_kv"], t), extra["kv"][:, u, :]).then_inc(sem, 16)
                sp.dma_start(node_rows(scratch["L1_q"], t), extra["q"][:, u, :]).then_inc(sem, 16)
            return 2

        rows_of(kit, "L1_table", [(xn, wkv, bkv, 2 * D), (xn, wq, bq, D)], finish, sink=sink, setup=setup)
    with Memory(kit) as m:
        acc, mx = m("L1_acc", [P, NT, 264]), m("L1_mx", [P, NT, 8])
        edge_pass(kit, "L1_edges", "dot", slots, buckets, scratch["L1_kv"], R_OTHER, scratch["L1_q"], 8, 33, acc, mx)
        rows = m("L1_rows", [P, NT, D])
        finish_softmax(kit, "L1_finish", acc, 8, 33, rows)
        sums = m("L1_sums", [P, 2, NP])
        turn_rows(kit, "L1_turn", rows, sums)
        wo, bo = m.loaded("L1_wo", "L1_bo")
        layers(kit, "L1_add", [Layer(wo, sums, x, bias=bo, add=True)])
    with Memory(kit) as m:
        wq, wk, wv, wo, bo = m.loaded("L1_mq", "L1_mk", "L1_mv", "L1_mo", "L1_mb")
        q, k, total = m("L1_mix_q", [P, 1, NP]), m("L1_mix_k", [P, 1, NP]), m("L1_total", [P, 1])
        ctx, a = m("L1_ctx", [P, 1, P]), m("L1_a", [P, 1, CW])
        layers(kit, "L1_mix_qk", [Layer(wq, xn, q, scale=32.0 ** -0.5), Layer(wk, xn, k)])
        soft_keys(kit, "L1_keys", k, total)
        context(kit, "L1_context", k, kit.ident[:].unsqueeze(1), xn, wv, 1, ctx, False, col_scale=total)
        layers(kit, "L1_mix_out", [Layer(ctx, q, a), Layer(wo, a, x, bias=bo, add=True)])
    layernorm(kit, "L1_norm2", x, xn)
    with Memory(kit) as m:
        comb_t = m("L1_comb_t", [P, NP])
        with Memory(kit) as m2:
            wr, br = m2.loaded("L1_wr", "L1_br")
            weight, comb = m2("L1_weight", [P, 1, NP]), m2("L1_comb", [P, NT, 8])
            layers(kit, "L1_weights", [Layer(wr, xn, weight, bias=br)])
            choose_half(kit, "L1_choose", weight[:, 0, :], comb, max(1, N // 2) - 1)
            clear(kit, "L1_clear", comb_t)
            turn_rows(kit, "L1_comb_turn", comb, comb_t[0:8, :])
        w1, w2, b1, b2 = m.loaded("L1_w1", "L1_w2", "L1_b1", "L1_b2")
        experts(kit, "L1_ffn", xn, x, [w1, w2], [b1], b2, comb_t, ACT.Gelu_apprx_tanh)
    add_in(kit, "L1_skip", x, xn)


def layer2(kit, x, xn, slots, buckets, scratch):
    nc = kit.nc
    layernorm(kit, "L2_norm", x, xn)
    for r in range(2):
        with Memory(kit) as m:
            w, b, brow = m.loaded(f"L2_wr{r}", f"L2_br{r}", f"L2_brow{r}")
            h = m(f"L2_h{r}", [P, 2, NP])

            def finish(dve, link, t, u, banks, extra):
                return nc.vector.tensor_scalar(extra["row"][:, u, :], banks[0][:, 0:D], 0.0, None, ALU.max)

            def sink(sp, t, u, extra, sem=None):
                if sp is not None:
                    sp.dma_start(node_rows(scratch["L2"], t, r * NP), extra["row"][:, u, :]).then_inc(sem, 16)
                return 1

            layers(kit, f"L2_rel{r}", [Layer(w, xn, h, bias=b, func="relu")])
            rows_of(kit, f"L2_table{r}", [(h, w, brow, D)], finish, sink=sink,
                    setup=lambda s: {"row": s.sb("row", [P, 2, D])})
    with Memory(kit) as m:
        agg = m("L2_agg", [P, 2, NP])
        with Memory(kit) as m2:
            acc = m2("L2_acc", [P, NT, D])
            edge_pass(kit, "L2_edges", "sum", slots, buckets, scratch["L2"], R_REL, None, 1, D, acc, None)
            turn_rows(kit, "L2_turn", acc, agg)
        wih, bih = m.loaded("L2_wih", "L2_bih")
        hn = m("L2_hn", [P, 2, NP])
        gates(kit, "L2_gates", agg, wih, bih, hn)
        w1, b1, w2, b2, w3, b3 = m.loaded("L2_w1", "L2_b1", "L2_w2", "L2_b2", "L2_w3", "L2_b3")
        h1, h2 = m("L2_head_h1", [P, 1, CW]), m("L2_head_h2", [P, 1, CW])
        layers(kit, "L2_head", [Layer(w1, hn, h1, bias=b1, func="relu"), Layer(w2, h1, h2, bias=b2, func="relu"),
                                Layer(w3, h2, x, bias=b3, add=True)])
    with Memory(kit) as m:
        wq, wk, wv, wo, gamma = m.loaded("L2_mq", "L2_mk", "L2_mv", "L2_mo", "L2_mg")
        q_t, k, total = m("L2_mix_q", [P, 2, NP]), m("L2_mix_k", [P, 2, NP]), m("L2_total", [P, 2])
        ctx, a = m("L2_ctx", [P, 2, D]), m("L2_a", [P, 2, CW])
        q = m("L2_q_rows", [P, NT, D])

        def finish_q(dve, link, t, u, banks, extra):
            return nc.vector.tensor_scalar(q[:, ds(t, 1), :].squeeze(1), banks[0][:, 0:D], 0.0, None, ALU.add)

        rows_of(kit, "L2_queries", [(xn, wq, None, D)], finish_q)
        softmax_queries(kit, "L2_soft_q", q, q)
        turn_rows(kit, "L2_q_turn", q, q_t)
        layers(kit, "L2_mix_keys", [Layer(wk, xn, k)])
        soft_keys(kit, "L2_keys", k, total)
        ident2, = m.loaded("ident2")
        context(kit, "L2_context", k, ident2, xn, wv, 2, ctx, False, col_scale=total, scale=32.0 ** -0.5)
        layers(kit, "L2_mix_out", [Layer(ctx, q_t, a), Layer(wo, a, k)])
        layernorm(kit, "L2_mix_norm", k, None, gamma=gamma, add_to=x)
    layernorm(kit, "L2_norm2", x, xn)
    with Memory(kit) as m:
        comb_t = m("L2_comb_t", [P, NP])
        with Memory(kit) as m2:
            rw, = m2.loaded("L2_rw")
            route(kit, "L2", m2, xn, rw, None, 8, comb_t, True)
        e1, e2, eb1, eb2 = m.loaded("L2_e1", "L2_e2", "L2_eb1", "L2_eb2")
        experts(kit, "L2_experts", xn, x, [e1, e2], [eb1], eb2, comb_t, ACT.Gelu)
    add_in(kit, "L2_skip", x, xn)


def attend(kit, name, j, heads, src, slots, buckets, table, key_table, rows):
    nc = kit.nc
    V = D // heads + 1
    F = heads * V
    with Memory(kit) as m:
        own = m(f"{name}_own", [P, NT, heads])
        with Memory(kit) as m2:
            w, a_src, a_dst = m2.loaded(f"L3_g{j}", f"L3_as{j}", f"L3_ad{j}")
            s_src, s_dst = m2(f"{name}_ssrc", [P, NT, heads]), m2(f"{name}_sdst", [P, NT, heads])

            def setup(s):
                row = s.sb("row", [P, 2, F + heads])
                return {"row": row, "key": s.sb("key", [P, 2, heads]), "prod": s.sb("prod", [P, 2, D]), "ones": [row[:]]}

            def finish(dve, link, t, u, banks, extra):
                row, prod = extra["row"][:, u, :], extra["prod"]
                nc.vector.tensor_copy(row[:, 0:F].rearrange("p (h v) -> p h v", h=heads)[:, :, 0:V - 1],
                                      banks[0][:, 0:D].rearrange("p (h v) -> p h v", h=heads))
                nc.vector.tensor_tensor(prod[:, 0, :], banks[0][:, 0:D], a_src, ALU.mult)
                link(nc.vector.tensor_tensor(prod[:, 1, :], banks[0][:, 0:D], a_dst, ALU.mult))
                both = prod[:].rearrange("p a (h v) -> p (a h) v", h=heads)
                nc.vector.tensor_reduce(row[:, F:F + heads], both[:, 0:heads], X, ALU.add)
                link(nc.vector.tensor_reduce(extra["key"][:, u, :], both[:, heads:2 * heads], X, ALU.add))
                nc.vector.tensor_scalar(s_src[:, ds(t, 1), :].squeeze(1), row[:, F:F + heads], 0.0, None, ALU.add)
                return nc.vector.tensor_scalar(s_dst[:, ds(t, 1), :].squeeze(1), extra["key"][:, u, :], 0.0, None,
                                               ALU.add)

            def sink(sp, t, u, extra, sem=None):
                if sp is not None:
                    sp.dma_start(node_rows(table, t), extra["row"][:, u, :]).then_inc(sem, 16)
                    sp.dma_start(node_rows(key_table, t), extra["key"][:, u, :]).then_inc(sem, 16)
                return 2

            rows_of(kit, f"{name}_table", [(src, w, None, D)], finish, sink=sink, setup=setup, links=2)
            own_scores(kit, f"{name}_own_scores", s_src, s_dst, own)
        acc, mx = m(f"{name}_acc", [P, NT, F]), m(f"{name}_mx", [P, NT, heads])
        edge_pass(kit, f"{name}_edges", "add", slots, buckets, table, R_OTHER, key_table, heads, V, acc, mx)
        finish_softmax(kit, f"{name}_finish", acc, heads, V, rows, mx=mx, own_score=own, own_dram=table)


def own_scores(kit, name, a, b, out):
    nc = kit.nc
    with Stage(kit, name) as s:
        chain = s.sem("chain")
        with nc.Block() as block:

            @block.vector
            def _(dve):
                link = Chain(dve, chain)
                link(nc.vector.tensor_tensor(out, a, b, ALU.add))
                nc.vector.scalar_tensor_tensor(out=out, in0=out, scalar=0.2, in1=out, op0=ALU.mult, op1=ALU.max)


def layer3(kit, x, xn, slots, buckets, scratch):
    nc = kit.nc
    layernorm(kit, "L3_norm", x, xn)
    with Memory(kit) as m:
        rows, gb1, gb2 = m("L3_rows", [P, NT, D]), *m.loaded("L3_gb1", "L3_gb2")
        attend(kit, "L3a", 1, 4, xn, slots, buckets, scratch["L3a"], scratch["L3a_key"], rows)
        with Memory(kit) as m2:
            h = m2("L3_h", [P, 2, NP])
            turn_rows(kit, "L3_h_turn", rows, h, bias=gb1)
            elu_in_place(kit, "L3_elu", h)
            attend(kit, "L3b", 2, 1, h, slots, buckets, scratch["L3b"], scratch["L3b_key"], rows)
        turn_rows(kit, "L3_add", rows, x, add=True, bias=gb2)
    with Memory(kit) as m:
        wq, wk, wv, wm, w1, w2, g1, b1, g2, b2 = m.loaded(
            "L3_mq", "L3_mk", "L3_mv", "L3_mm", "L3_m1", "L3_m2", "L3_g1c", "L3_b1c", "L3_g2c", "L3_b2c")
        msg = m("L3_msg", [P, 2, NP])
        with Memory(kit) as m2:
            linear_attention(kit, "L3_mix", m2, xn, wq, wk, wv, floor=-3e38, plus=1e-6, shrink=float(N),
                             out=lambda a: [Layer(wm, a, msg)])
        layernorm(kit, "L3_msg_norm", msg, msg)
        stretch(kit, "L3_msg_stretch", msg, g1, b1)
        h = m("L3_mh", [P, 4, CW])
        out = m("L3_mout", [P, 2, NP])
        layers(kit, "L3_mix_mlp", [Layer(w1, (xn, msg), h, func="relu"), Layer(w2, h, out)])
        layernorm(kit, "L3_out_norm", out, None, gamma=g2, add_to=x)
        add_in(kit, "L3_mix_skip", x, xn, bias=b2)
    layernorm(kit, "L3_norm2", x, xn)
    with Memory(kit) as m:
        back, scale = m("L3_back", [P, NT], U32), m("L3_scale", [P, NT])
        with Memory(kit) as m2:
            place = m2("L3_place", [P, NT], U32)
            gw, gb, ident2 = m2.loaded("L3_gw", "L3_gateb", "ident2")
            logits, rows = m2("L3_logits", [P, NT, EXPERTS]), m2("L3_given", [P, NT, D])

            def finish(dve, link, t, u, banks, extra):
                nc.vector.tensor_scalar(logits[:, ds(t, 1), :].squeeze(1), banks[0][:, 0:EXPERTS], 0.0, None, ALU.add)
                return nc.vector.tensor_scalar(rows[:, ds(t, 1), :].squeeze(1), banks[1][:, 0:D], 0.0, None, ALU.add)

            rows_of(kit, "L3_logit_rows", [(xn, gw, gb, EXPERTS), (xn, ident2, None, D)], finish)
            assign(kit, "L3_assign", logits, place, back, scale)
            move_rows(kit, "L3_give", rows, scratch["given"], place, True)
        run_experts(kit, "L3_experts", scratch["given"], scratch["made"])
        rows = m("L3_taken", [P, NT, D])
        move_rows(kit, "L3_take", rows, scratch["made"], back, False)
        scale_rows(kit, "L3_weigh", rows, scale)
        turn_rows(kit, "L3_out", rows, x, add=True)


SCRATCH = {
    "by_dst": ((NSLOT + DUMP, REC), I32), "by_src": ((NSLOT + DUMP, REC), I32),
    "L0": ((NP, 136), F32), "L1_kv": ((NP, 520), F32), "L1_q": ((NP, D), F32), "L2": ((2 * NP, D), F32),
    "L3a": ((NP, 264), F32), "L3a_key": ((NP, 4), F32), "L3b": ((NP, 258), F32), "L3b_key": ((NP, 1), F32),
    "given": ((2 * EXPERTS * CAPT * P, D), F32), "made": ((EXPERTS * CAPT * P, D), F32),
}


def program(nc, dram, out):
    kit = Kit(nc, dram)
    scratch = {n: nc.dram_tensor(f"scratch_{n}", shape, dt).ap() for n, (shape, dt) in SCRATCH.items()}
    with ExitStack() as ctx:
        constants(kit, ctx)
        x = ctx.enter_context(nc.sbuf_tensor("x", [P, 2, NP], F32))[:]
        by_dst = ctx.enter_context(nc.sbuf_tensor("bucket_by_dst", [1, ST], I32))[:]
        by_src = ctx.enter_context(nc.sbuf_tensor("bucket_by_src", [1, ST], I32))[:]
        sort_edges(kit, "sort_dst", dram["dst"], dram["src0"], scratch["by_dst"], by_dst)
        sort_edges(kit, "sort_src", dram["src"], dram["dst0"], scratch["by_src"], by_src)
        load(kit, "load_x", [(x, dram["x"])])
        xn = ctx.enter_context(nc.sbuf_tensor("xn", [P, 2, NP], F32))[:]
        layer0(kit, x, xn, scratch["by_dst"], by_dst, scratch)
        layer1(kit, x, xn, scratch["by_src"], by_src, scratch)
        layer2(kit, x, xn, scratch["by_dst"], by_dst, scratch)
        layer3(kit, x, xn, scratch["by_dst"], by_dst, scratch)
        load(kit, "store", [(out, x)])


def halves(w):
    *lead, k, n = w.shape
    return np.ascontiguousarray(np.moveaxis(w.reshape(*lead, k // P, P, n), -2, -3))


def column(b):
    *lead, n = b.shape
    return np.ascontiguousarray(np.swapaxes(b.reshape(*lead, n // P, P), -1, -2))


def edge_layout(a, fill):
    out = np.full((P * ET,), fill, a.dtype)
    out[:E] = a
    return out.reshape(P, ET)


def layout(inputs):
    a = {k: np.asarray(v) for k, v in inputs.items()}
    o = {}
    x = np.zeros((NP, D), np.float32)
    x[:N] = a["x"]
    o["x"] = np.ascontiguousarray(x.T.reshape(2, P, NP).transpose(1, 0, 2))
    o["src"] = edge_layout(a["src"], -1)
    o["dst"] = edge_layout(a["dst"], -1)
    o["src0"] = edge_layout(a["src"], 0)
    o["dst0"] = edge_layout(a["dst"], 0)
    o["edge_type"] = edge_layout(a["edge_type_2"], 0)
    o["edge_attr"] = np.ascontiguousarray(
        np.stack([edge_layout(a["edge_attr_2"][:, j], 0) for j in range(2)], 1))
    q, t = np.arange(P)[:, None], np.arange(ET)[None]
    o["spill"] = np.where(q < EFULL, 0, NSLOT + (P - EFULL) * t + q - EFULL).astype(np.float32)
    r = np.arange(P)
    o["ident"] = np.eye(P, dtype=np.float32)
    o["iota"] = np.tile(r.astype(np.float32), (P, 1))
    o["earlier"] = (r[None] < r[:, None]).astype(np.float32)
    o["later"] = (r[None] > r[:, None]).astype(np.float32)
    o["tile_no"] = np.tile(np.arange(ST, dtype=np.float32), (P, 1))
    o["heads"] = (r[None] // 32 == r[:, None] // 32).astype(np.float32)
    o["pick"] = np.ascontiguousarray(np.broadcast_to(np.eye(P, 8, dtype=np.float32)[:, :, None], (P, 8, P)))
    o["ident2"] = halves(np.eye(D, dtype=np.float32))
    node = np.arange(NP).reshape(NT, P).T
    o["node_real"] = (node < N).astype(np.float32)
    o["node_spare"] = (node + EXPERTS * CAPT * P).astype(np.float32)
    weights(a, o)
    return o


def flat(b):
    return np.ascontiguousarray(b.reshape(1, -1))


def per_expert(w):
    return np.ascontiguousarray(np.moveaxis(halves(w), 0, 1))


def wide(b):
    return np.ascontiguousarray(np.broadcast_to(b.reshape(1, -1), (P, b.size)))


def padded(b, n=P):
    out = np.zeros((n, b.shape[-1]), b.dtype)
    out[:b.shape[0]] = b
    return out


def weights(a, o):
    L = "L0_gnn_"
    o["L0_w_fwd"], o["L0_w_rev"] = halves(a[L + "W_forward"].T), halves(a[L + "W_reverse"].T)
    o["L0_w_rows"] = np.ascontiguousarray(np.stack([a[L + "W_forward"], a[L + "W_reverse"]], 1))
    o["L0_attn"] = np.ascontiguousarray(a[L + "attn_forward"][0].T)
    L = "L0_mix_"
    o["L0_wq"], o["L0_wk"], o["L0_wv"] = (halves(w.T) for w in (a[L + "Wq"], a[L + "Wkv"][:D], a[L + "Wkv"][D:]))
    o["L0_wp"], o["L0_bp"] = halves(a[L + "Wproj"].T), column(a[L + "bproj"])
    L = "L0_ffn_"
    o["L0_r1"], o["L0_rb1"] = halves(a[L + "router_w1"]), column(a[L + "router_b1"])
    o["L0_r2"], o["L0_rb2"] = halves(a[L + "router_w2"]), flat(a[L + "router_b2"])
    for j in (1, 2, 3):
        o[f"L0_e{j}"] = per_expert(a[L + f"expert_w{j}"])
    for j in (1, 2):
        o[f"L0_eb{j}"] = np.ascontiguousarray(np.moveaxis(column(a[L + f"expert_b{j}"]), 0, 1))
    o["L0_eb3"] = padded(a[L + "expert_b3"])
    head = np.arange(D).reshape(32, 8).T.ravel()
    L = "L1_gnn_"
    o["L1_wq"] = halves(a[L + "Wq"].T[:, head])
    o["L1_wkv"] = halves(np.concatenate([a[L + "Wk"].T[:, head], a[L + "Wv"].T[:, head]], 1))
    o["L1_bq"] = flat(a[L + "bq"][head])
    o["L1_bkv"] = flat(np.concatenate([a[L + "bk"][head], a[L + "bv"][head]]))
    o["L1_wo"], o["L1_bo"] = halves(a[L + "Wo"].T[head]), column(a[L + "bo"])
    L = "L1_mix_"
    for j, n in enumerate(("q", "k", "v")):
        o[f"L1_m{n}"] = halves(a[L + "W_qkv"][:, j * P:(j + 1) * P])
    o["L1_mo"], o["L1_mb"] = halves(a[L + "W_out"]), column(a[L + "b_out"])
    L = "L1_ffn_"
    o["L1_wr"] = halves(np.ascontiguousarray(np.broadcast_to(a[L + "wr"], (D, P))))
    o["L1_br"] = np.ascontiguousarray(np.broadcast_to(a[L + "br"].reshape(1, 1), (P, 1)))
    o["L1_w1"], o["L1_w2"] = per_expert(a[L + "w1"][None]), per_expert(a[L + "w2"][None])
    o["L1_b1"] = np.ascontiguousarray(column(a[L + "b1"])[:, None])
    o["L1_b2"] = padded(a[L + "b2"][None])
    L = "L2_gnn_"
    for r in range(2):
        o[f"L2_wr{r}"] = halves(a[L + "W_rel"][r].T)
        o[f"L2_br{r}"], o[f"L2_brow{r}"] = column(a[L + "b_rel"][r]), flat(a[L + "b_rel"][r])
    used = np.r_[0:D, 2 * D:4 * D]
    o["L2_wih"] = halves(a[L + "W_ih"].T[:, used])
    o["L2_bih"] = np.ascontiguousarray(np.stack([column(a[L + "b_ih"][used]), column(a[L + "b_hh"][used])], 1))
    for j in (1, 2, 3):
        o[f"L2_w{j}"], o[f"L2_b{j}"] = halves(a[L + f"W{j}"].T), column(a[L + f"b{j}"])
    L = "L2_mix_"
    for j, n in enumerate(("q", "k", "v")):
        o[f"L2_m{n}"] = halves(a[L + "Wqkv"][:, j * D:(j + 1) * D])
    o["L2_mo"], o["L2_mg"] = halves(a[L + "Wout"]), column(a[L + "gamma"])
    L = "L2_ffn_"
    o["L2_rw"] = halves(a[L + "router_w"].T)
    for j in (1, 2):
        o[f"L2_e{j}"] = per_expert(a[L + f"w{j}"])
    o["L2_eb1"] = np.ascontiguousarray(np.moveaxis(column(a[L + "b1"]), 0, 1))
    o["L2_eb2"] = padded(a[L + "b2"])
    L = "L3_gnn_"
    for j in (1, 2):
        o[f"L3_g{j}"], o[f"L3_gb{j}"] = halves(a[L + f"W{j}"]), column(a[L + f"b{j}"])
        o[f"L3_as{j}"], o[f"L3_ad{j}"] = wide(a[L + f"a_src{j}"]), wide(a[L + f"a_dst{j}"])
    L = "L3_mix_"
    for n in ("q", "k", "v", "m", "1", "2"):
        o[f"L3_m{n}"] = halves(a[L + "W" + n])
    for n in ("g1", "b1", "g2", "b2"):
        o[f"L3_{n}c"] = column(a[L + n])
    L = "L3_ffn_"
    o["L3_gw"], o["L3_gateb"] = halves(a[L + "gate_w"]), flat(a[L + "gate_b"])
    o["L3_w1"], o["L3_w2"] = halves(a[L + "w1"]), halves(a[L + "w2"])
    o["L3_b1"], o["L3_b2"] = column(a[L + "b1"]), np.ascontiguousarray(a[L + "b2"][:, None])


def kernel(**inputs):
    import concourse.bacc as bacc
    from concourse.bass_utils import run_bass_kernel_spmd

    arrays = {f"in_{k}": v for k, v in layout(inputs).items()}
    nc = bacc.Bacc("TRN2", target_bir_lowering=False, num_devices=1)
    dram = {k[3:]: nc.dram_tensor(k, v.shape, mybir.dt.from_np(v.dtype), kind="ExternalInput").ap()
            for k, v in arrays.items()}
    out = nc.dram_tensor("out", (P, 2, NP), F32, kind="ExternalOutput").ap()
    program(nc, dram, out)
    got = run_bass_kernel_spmd(nc, [arrays], core_ids=[0]).results[0]["out"]
    return np.ascontiguousarray(got.transpose(2, 1, 0).reshape(NP, D)[:N])
```
